# Optimizing a Trainium2 kernel written in Bass

```python
import numpy as np
import jax
import jax.numpy as jnp

def _softmax(x, axis=-1):
    return jax.nn.softmax(x, axis=axis)

def _gelu(x):
    return jax.nn.gelu(x, approximate=True)

def _silu(x):
    return jax.nn.silu(x)

def _sigmoid(x):
    return jax.nn.sigmoid(x)

def _layernorm(x, axis=-1, eps=1e-05):
    m = jnp.mean(x, axis=axis, keepdims=True)
    v = jnp.var(x, axis=axis, keepdims=True)
    return (x - m) / jnp.sqrt(v + eps)

def _scatter_add(tgt, idx, src, axis=0):
    return tgt.at[idx].add(src)

def _segment_sum(src, seg, n):
    return jax.ops.segment_sum(src, seg, n)
kernel_name = 'mk_decoder_postln_d1_seqx_r4_df276a'

def setup_inputs(seed: int=0):
    np.random.seed(seed)
    _w = jnp.asarray

    def _rec_inputs():
        import jax
        import jax.numpy as jnp
        _rk = jax.random.key(seed)
        x = -0.0003929 + 0.9999 * jax.random.normal(jax.random.fold_in(_rk, 1), (32, 256, 256), jnp.float32)
        _lenS = 256 - jax.random.randint(jax.random.fold_in(_rk, 7), (32,), 0, max(1, 256 // 4) + 1, jnp.int32)
        _lenS2 = 120 - jax.random.randint(jax.random.fold_in(_rk, 8), (32,), 0, max(1, 120 // 4) + 1, jnp.int32)
        _ctx_1024P = jax.random.normal(jax.random.fold_in(_rk, 11), (32, 16, 256), jnp.float32)
        _ctx_1024c = jax.random.dirichlet(jax.random.fold_in(_rk, 511), 0.3 * jnp.ones((16,), jnp.float32), (32, 120))
        _ctx_1024t = jnp.einsum('bsk,bkd->bsd', _ctx_1024c, _ctx_1024P)
        _ctx_1024t = _ctx_1024t * jax.lax.rsqrt(jnp.mean(jnp.square(_ctx_1024t)) + 1e-12) * 0.953939
        ctx_1024 = 2.81802e-05 + 1.00001 * (_ctx_1024t + 0.3 * jax.random.normal(jax.random.fold_in(_rk, 611), (32, 120, 256), jnp.float32))
        _validS = jnp.arange(256)[None, :] < _lenS[:, None]
        _validS2 = jnp.arange(120)[None, :] < _lenS2[:, None]
        _causal = jnp.tril(jnp.ones((256, 256), dtype=bool))
        mask_S2_ik0 = jnp.where(_validS2[0], 0, 1).astype(jnp.int32)
        return (x, ctx_1024, mask_S2_ik0)
    x, ctx_1024, mask_S2_ik0 = _rec_inputs()

    def _L0_attn_setup():
        import jax, jax.numpy as jnp
        import numpy as np
        import math
        D_MODEL = 256
        N_HEADS = 16
        D_HEAD = D_MODEL // N_HEADS
        LSR_RANK = 32
        B, T = (4, 512)
        key = jax.random.key(seed)
        ks = jax.random.split(key, 11)
        s = 1.0 / math.sqrt(D_MODEL)
        x = jax.random.normal(ks[0], (B, T, D_MODEL), dtype=jnp.float32)
        Wq = jax.random.uniform(ks[1], (D_MODEL, D_MODEL), minval=-s, maxval=s)
        bq = jax.random.uniform(ks[2], (D_MODEL,), minval=-s, maxval=s)
        Wk = jax.random.uniform(ks[3], (D_MODEL, D_MODEL), minval=-s, maxval=s)
        bk = jax.random.uniform(ks[4], (D_MODEL,), minval=-s, maxval=s)
        Wv = jax.random.uniform(ks[5], (D_MODEL, D_MODEL), minval=-s, maxval=s)
        bv = jax.random.uniform(ks[6], (D_MODEL,), minval=-s, maxval=s)
        Wo = jax.random.uniform(ks[7], (D_MODEL, D_MODEL), minval=-s, maxval=s)
        bo = jax.random.uniform(ks[8], (D_MODEL,), minval=-s, maxval=s)
        Wq_lsr = jax.random.normal(ks[9], (N_HEADS, D_HEAD, LSR_RANK)) / math.sqrt(D_HEAD)
        Wk_lsr = jax.random.normal(ks[10], (N_HEADS, D_HEAD, LSR_RANK)) / math.sqrt(D_HEAD)
        return {'x': x, 'Wq': Wq, 'bq': bq, 'Wk': Wk, 'bk': bk, 'Wv': Wv, 'bv': bv, 'Wo': Wo, 'bo': bo, 'Wq_lsr': Wq_lsr, 'Wk_lsr': Wk_lsr}
    _L0_attn_all = _L0_attn_setup()
    _L0_attn_in = {k: v for k, v in _L0_attn_all.items() if k in ('Wq', 'bq', 'Wk', 'bk', 'Wv', 'bv', 'Wo', 'bo', 'Wq_lsr', 'Wk_lsr')}
    del _L0_attn_all

    def _L0_xattn_setup():
        import jax, jax.numpy as jnp
        import numpy as np
        DIM = 256
        NUM_HEADS = 8
        SCALE = (DIM // NUM_HEADS) ** (-0.5)
        key = jax.random.key(seed)
        k1, k2, k3, k4, k5, k6 = jax.random.split(key, 6)
        B, N, M, C = (8, 512, 512, DIM)
        x = jax.random.normal(k1, (B, N, C), dtype=jnp.float32)
        support = jax.random.normal(k2, (B, M, C), dtype=jnp.float32)
        attn_mask = jax.random.randint(k3, (M,), 0, 2, dtype=jnp.int32)
        qkv_w = jax.random.normal(k4, (3 * C, C), dtype=jnp.float32) * C ** (-0.5)
        proj_w = jax.random.normal(k5, (C, C), dtype=jnp.float32) * C ** (-0.5)
        proj_b = jax.random.normal(k6, (C,), dtype=jnp.float32) * 0.01
        return {'x': x, 'support': support, 'attn_mask': attn_mask, 'qkv_w': qkv_w, 'proj_w': proj_w, 'proj_b': proj_b}
    _L0_xattn_all = _L0_xattn_setup()
    _L0_xattn_in = {k: v for k, v in _L0_xattn_all.items() if k in ('qkv_w', 'proj_w', 'proj_b')}
    del _L0_xattn_all

    def _L0_ffn_setup():
        import jax, jax.numpy as jnp
        import numpy as np
        DIM = 256

        def _reference_tuple_inner(x, W_r, W_k, W_v, mu_r, mu_k):
            B, T, C = x.shape
            x_prev = jnp.concatenate([jnp.zeros((B, 1, C), x.dtype), x[:, :-1, :]], axis=1)
            xr = mu_r * x + (1.0 - mu_r) * x_prev
            xk = mu_k * x + (1.0 - mu_k) * x_prev
            r = jax.nn.sigmoid(jnp.einsum('btc,dc->btd', xr, W_r))
            k = jnp.einsum('btc,dc->btd', xk, W_k)
            k_act = jnp.square(jax.nn.relu(k))
            out = r * jnp.einsum('btc,dc->btd', k_act, W_v)
            new_state = x[:, -1, :]
            return (out, new_state)
        key = jax.random.key(seed)
        ks = jax.random.split(key, 6)
        B, T, C = (8, 512, DIM)
        x = jax.random.normal(ks[0], (B, T, C), dtype=jnp.float32)
        s = 1.0 / np.sqrt(C)
        W_r = jax.random.uniform(ks[1], (C, C), jnp.float32, -s, s)
        W_k = jax.random.uniform(ks[2], (C, C), jnp.float32, -s, s)
        W_v = jax.random.uniform(ks[3], (C, C), jnp.float32, -s, s)
        mu_r = jax.random.uniform(ks[4], (C,), jnp.float32)
        mu_k = jax.random.uniform(ks[5], (C,), jnp.float32)
        return {'x': x, 'W_r': W_r, 'W_k': W_k, 'W_v': W_v, 'mu_r': mu_r, 'mu_k': mu_k}
    _L0_ffn_all = _L0_ffn_setup()
    _L0_ffn_in = {k: v for k, v in _L0_ffn_all.items() if k in ('W_r', 'W_k', 'W_v', 'mu_r', 'mu_k')}
    del _L0_ffn_all
    return {'x': x, 'ctx_1024': ctx_1024, 'mask_S2_ik0': mask_S2_ik0, 'L0_attn_Wq': _L0_attn_in['Wq'], 'L0_attn_bq': _L0_attn_in['bq'], 'L0_attn_Wk': _L0_attn_in['Wk'], 'L0_attn_bk': _L0_attn_in['bk'], 'L0_attn_Wv': _L0_attn_in['Wv'], 'L0_attn_bv': _L0_attn_in['bv'], 'L0_attn_Wo': _L0_attn_in['Wo'], 'L0_attn_bo': _L0_attn_in['bo'], 'L0_attn_Wq_lsr': _L0_attn_in['Wq_lsr'], 'L0_attn_Wk_lsr': _L0_attn_in['Wk_lsr'], 'L0_xattn_qkv_w': _L0_xattn_in['qkv_w'], 'L0_xattn_proj_w': _L0_xattn_in['proj_w'], 'L0_xattn_proj_b': _L0_xattn_in['proj_b'], 'L0_ffn_W_r': _L0_ffn_in['W_r'], 'L0_ffn_W_k': _L0_ffn_in['W_k'], 'L0_ffn_W_v': _L0_ffn_in['W_v'], 'L0_ffn_mu_r': _L0_ffn_in['mu_r'], 'L0_ffn_mu_k': _L0_ffn_in['mu_k']}

def reference(x, ctx_1024, mask_S2_ik0, L0_attn_Wq, L0_attn_bq, L0_attn_Wk, L0_attn_bk, L0_attn_Wv, L0_attn_bv, L0_attn_Wo, L0_attn_bo, L0_attn_Wq_lsr, L0_attn_Wk_lsr, L0_xattn_qkv_w, L0_xattn_proj_w, L0_xattn_proj_b, L0_ffn_W_r, L0_ffn_W_k, L0_ffn_W_v, L0_ffn_mu_r, L0_ffn_mu_k):
    import jax
    import jax.numpy as jnp

    def _L0_attn_ref(x, Wq, bq, Wk, bk, Wv, bv, Wo, bo, Wq_lsr, Wk_lsr):
        import jax, jax.numpy as jnp
        import numpy as np
        import math
        D_MODEL = 256
        N_HEADS = 16
        D_HEAD = D_MODEL // N_HEADS
        LSR_RANK = 32
        B, T = (4, 512)
        Bq, Tq, _ = x.shape

        def split_heads(y):
            return y.reshape(Bq, Tq, N_HEADS, D_HEAD).transpose(0, 2, 1, 3)
        q = split_heads(x @ Wq.T + bq)
        k = split_heads(x @ Wk.T + bk)
        v = split_heads(x @ Wv.T + bv)
        q_lr = jnp.einsum('bhtd,hdr->bhtr', q, Wq_lsr)
        k_lr = jnp.einsum('bhtd,hdr->bhtr', k, Wk_lsr)
        scale = 1.0 / math.sqrt(max(LSR_RANK, 1))
        scores = jnp.einsum('bhir,bhjr->bhij', q_lr, k_lr) * scale
        causal_mask = jnp.triu(jnp.ones((Tq, Tq), dtype=bool), k=1)
        scores = jnp.where(causal_mask, jnp.float32(-jnp.inf), scores)
        attn = jax.nn.softmax(scores, axis=-1)
        y = jnp.einsum('bhij,bhjd->bhid', attn, v)
        y = y.transpose(0, 2, 1, 3).reshape(Bq, Tq, D_MODEL)
        return y @ Wo.T + bo

    def _L0_xattn_ref(x, support, attn_mask, qkv_w, proj_w, proj_b):
        import jax, jax.numpy as jnp
        import numpy as np
        DIM = 256
        NUM_HEADS = 8
        SCALE = (DIM // NUM_HEADS) ** (-0.5)
        B, N, C = x.shape
        wq, wk, wv = (qkv_w[:C], qkv_w[C:2 * C], qkv_w[2 * C:])
        q = jnp.einsum('bnc,dc->bnd', x, wq)
        k = jnp.einsum('bmc,dc->bmd', support, wk)
        v = jnp.einsum('bmc,dc->bmd', support, wv)
        attn = jnp.einsum('bnd,bmd->bnm', q, k) * SCALE
        attn = jax.nn.softmax(attn, axis=-1)
        attn = jnp.where(attn_mask[None, None, :] == 0, 0.0, attn)
        out = jnp.einsum('bnm,bmd->bnd', attn, v)
        out = jnp.swapaxes(out, 1, 2).reshape(B, N, C)
        out = jnp.einsum('bnc,dc->bnd', out, proj_w) + proj_b
        return out

    def _L0_ffn_ref(x, W_r, W_k, W_v, mu_r, mu_k):
        import jax, jax.numpy as jnp
        import numpy as np
        DIM = 256

        def _reference_tuple_inner(x, W_r, W_k, W_v, mu_r, mu_k):
            B, T, C = x.shape
            x_prev = jnp.concatenate([jnp.zeros((B, 1, C), x.dtype), x[:, :-1, :]], axis=1)
            xr = mu_r * x + (1.0 - mu_r) * x_prev
            xk = mu_k * x + (1.0 - mu_k) * x_prev
            r = jax.nn.sigmoid(jnp.einsum('btc,dc->btd', xr, W_r))
            k = jnp.einsum('btc,dc->btd', xk, W_k)
            k_act = jnp.square(jax.nn.relu(k))
            out = r * jnp.einsum('btc,dc->btd', k_act, W_v)
            new_state = x[:, -1, :]
            return (out, new_state)
        return _reference_tuple_inner(x, W_r, W_k, W_v, mu_r, mu_k)[0]
    x = _layernorm(x + _L0_attn_ref(x, L0_attn_Wq, L0_attn_bq, L0_attn_Wk, L0_attn_bk, L0_attn_Wv, L0_attn_bv, L0_attn_Wo, L0_attn_bo, L0_attn_Wq_lsr, L0_attn_Wk_lsr), axis=-1)
    x = _layernorm(x + _L0_xattn_ref(x, ctx_1024, mask_S2_ik0, L0_xattn_qkv_w, L0_xattn_proj_w, L0_xattn_proj_b), axis=-1)
    x = _layernorm(x + _L0_ffn_ref(x, L0_ffn_W_r, L0_ffn_W_k, L0_ffn_W_v, L0_ffn_mu_r, L0_ffn_mu_k), axis=-1)
    return x

_drawn_inputs = setup_inputs


def setup_inputs(seed=0):
    import zlib

    import numpy as np

    out = dict(_drawn_inputs(seed))
    spreads = {}
    factors = {'L0_attn_Wq': 3.397,
     'L0_attn_bq': 8.0,
     'L0_attn_Wk': 3.34,
     'L0_attn_bk': 8.0,
     'L0_attn_bv': 2.756,
     'L0_attn_Wq_lsr': 3.342,
     'L0_attn_Wk_lsr': 3.379,
     'L0_xattn_proj_b': 5.395,
     'L0_ffn_W_r': 3.18,
     'L0_ffn_mu_r': 6.415}
    for name, (base, spread) in spreads.items():
        noise = np.random.default_rng([zlib.crc32(name.encode()), seed]).standard_normal(out[name].shape)
        drawn = base * np.exp(spread * noise) if base else spread * noise
        out[name] = jnp.asarray(drawn.astype(out[name].dtype))
    for name, factor in factors.items():
        out[name] = (out[name] * factor).astype(out[name].dtype)
    return out
```

```python
from contextlib import ExitStack

import concourse.bass as bass
from concourse import mybir

F32 = mybir.dt.float32
F32R = mybir.dt.float32r
BF16 = mybir.dt.bfloat16
F16 = mybir.dt.float16
I32 = mybir.dt.int32
ALU = mybir.AluOpType
ACT = mybir.ActivationFunctionType
AX_X = mybir.AxisListType.X

P = 128
RING = 3
HEADS, DH, RANK = 16, 16, 32
EPS = 1e-5
MASKED = -1e30
LN2_12 = 8.317766166719343
XATTN_HEADS = 8

IN, SCORES, PROBS, CROSS, FFN = range(5)
LAST_SKEW = FFN
ONES_ROW = 48
STACK_ROWS = ONES_ROW + 2


class Batch:

    def __init__(self, turn, at, skew):
        self.n = 3 * turn + (at - skew)
        self.slot = (at - skew) % RING
        self.turn = turn + (at - skew) // RING
        self.static = isinstance(turn, int)

    def dma_count(self, dmas, back=0):
        return (self.turn + (1 - back)) * (16 * dmas)


def decoder_layer(nc, x, ctx_in, mask_in, Wq, bq, Wk, bk, Wv, bv, Wo, bo, Wq_lsr, Wk_lsr,
                  qkv_w, proj_w, proj_b, W_r, W_k, W_v, mu_r, mu_k, out):
    B, T, C = x.shape
    M = ctx_in.shape[1]
    NT, KC = T // P, C // P
    XSCALE = float(C // XATTN_HEADS) ** -0.5
    assert NT == 2 and KC == 2 and M <= P and C == HEADS * DH

    es = ExitStack()
    with es:
        def sb(name, shape, dt=F32):
            return es.enter_context(nc.sbuf_tensor(name, shape, dt))

        def ps(name, shape, dt=F32):
            return es.enter_context(nc.psum_tensor(name, shape, dt))

        def sem(name):
            return es.enter_context(nc.semaphore(name))

        ident = sb("ident", [P, P])
        identb = sb("identb", [P, P], BF16)
        mask_s = sb("mask_s", [P, 4, P], BF16)
        mask_t = sb("mask_t", [P, 4, P], BF16)
        block_diag = sb("block_diag", [P, P])
        ones_row = sb("ones_row", [1, P])
        neg_half = sb("neg_half", [P, NT])
        eps = sb("eps", [P, NT])
        pause = sb("pause", [P, 1])
        raw_names = ["Wq", "Wk", "Wv", "Wo", "Wxq", "Wxk", "Wxv", "Wp", "Wr", "Wkf", "Wvf"]
        raw_dram = {"Wq": Wq, "Wk": Wk, "Wv": Wv, "Wo": Wo, "Wxq": qkv_w[0:C, :], "Wxk": qkv_w[C:2 * C, :],
                    "Wxv": qkv_w[2 * C:3 * C, :], "Wp": proj_w, "Wr": W_r, "Wkf": W_k, "Wvf": W_v}
        turned_names = ["Wk", "Wv", "Wo", "Wxv", "Wp", "Wr", "Wkf", "Wvf"]
        wT = {n: sb("T_" + n, [P, KC, C]) for n in turned_names}
        wq_fold = sb("wq_fold", [P, KC, C])
        wx_fold = sb("wx_fold", [P, KC, C])
        lsr = sb("lsr", [P, 2, KC, RANK])
        lsrT = sb("lsrT", [RANK, 2, KC, P])
        lsr_prod = sb("lsr_prod", [P, KC, P])
        cols = sb("cols", [P, 5, KC])
        BQ, BK, BV, MUR, MUK = range(5)
        bq_fold = sb("bq_fold", [P, KC])
        rows = sb("rows", [1, 2, C])
        bv_rep = sb("bv_rep", [P, KC, P])
        c1 = sb("c1", [P, C])
        pb_rep = sb("pb_rep", [P, C])
        mask_i = sb("mask_i", [M, 1], I32)
        keep = sb("keep", [M, 1])

        x_in = [sb(f"x_in{r}", [P, NT, C]) for r in range(RING)]
        xT = [sb(f"xT{r}", [P, KC, T]) for r in range(RING)]
        parts = [sb(f"parts{s}", [P, KC, 2, T], F32R) for s in range(2)]
        stack = [[sb(f"stack{s}_{r}", [P, HEADS // 2, T], F32R) for r in range(RING)] for s in range(2)]
        row_max = sb("row_max", [P, NT, 2, HEADS // 2])
        shift = sb("shift", [HEADS, T])
        shift_parts = sb("shift_parts", [HEADS, 2, T], F32R)
        v_parts = [sb(f"v_parts{r}", [P, NT, HEADS, 3, DH + 1], BF16) for r in range(RING)]
        v_rest = sb("v_rest", [P, NT, C])
        p32 = [sb(f"p32_{i}", [P, 1024]) for i in range(3)]
        p_hi = [sb(f"p_hi{i}", [P, 1024], F16) for i in range(6)]
        p_lo = [sb(f"p_lo{i}", [P, 1024], F16) for i in range(6)]
        raw = {n: t[:].bitcast(F32).rearrange("p (a c) -> p a c", a=KC) for n, t in zip(raw_names, p_hi + p_lo)}
        o_sum = sb("o_sum", [P, NT, HEADS // 2, DH + 1])
        o_rec = sb("o_rec", [P, NT, HEADS // 2])
        y = sb("y", [P, NT, HEADS, DH])
        yT = sb("yT", [P, KC, T])
        ctx_sb = sb("ctx_sb", [M, C])
        ctxT = sb("ctxT", [P, KC, M])
        kxT = [sb(f"kxT{r}", [P, KC, M]) for r in range(RING)]
        vx = [sb(f"vx{r}", [M, C]) for r in range(RING)]
        x_res = sb("x_res", [P, NT, C])
        x_c = sb("x_c", [P, NT, C])
        sum1 = sb("sum1", [P, NT, C])
        sum2 = sb("sum2", [P, NT, C])
        sum3 = sb("sum3", [P, NT, C])
        bn = [sb(f"bn{i}", [P, NT, 6]) for i in range(3)]
        mv = [sb(f"mv{i}", [P, NT, 2]) for i in range(3)]
        var = [sb(f"var{i}", [P, NT]) for i in range(3)]
        rstd = [sb(f"rstd{i}", [P, NT]) for i in range(3)]
        x1 = sb("x1", [P, NT, C])
        x1p = sb("x1p", [P, NT, C])
        x1T = sb("x1T", [P, KC, T])
        s2_max = sb("s2_max", [P, NT])
        s2_neg = sb("s2_neg", [P, NT])
        s2_sum = sb("s2_sum", [P, NT])
        s2_rec = sb("s2_rec", [P, NT])
        a_exp = sb("a_exp", [P, NT, M])
        a_nrm = sb("a_nrm", [P, NT, M])
        g_sb = sb("g_sb", [M, C])
        x2 = [sb(f"x2_{r}", [P, NT, C]) for r in range(RING)]
        x2T = sb("x2T", [P, KC, 1 + T])
        dx = sb("dx", [P, KC, T])
        xr = sb("xr", [P, KC, T])
        xk = sb("xk", [P, KC, T])
        k_relu = sb("k_relu", [P, KC, T])
        k_act = sb("k_act", [P, KC, T])
        r_tanh = sb("r_tanh", [P, NT, C])
        gated = sb("gated", [P, NT, C])
        x3 = sb("x3", [P, NT, C])

        parts_dram = [[nc.dram_tensor(f"parts_dram{s}_{r}", [KC * P, 2, T], F32, kind="Internal").ap()
                       for r in range(RING)] for s in range(2)]

        ps_s = ps("ps_s", [P, 1024])
        ps_t = ps("ps_t", [P, 1024])
        ps_o = ps("ps_o", [P, NT, 512])
        ps_m = [ps(f"ps_m{i}", [P, 512]) for i in range(2)]

        def sems(*names):
            return {n: sem(n) for n in names}

        filled = sems(*["f_" + n for n in ("xT", "q", "k", "v", "mT", "yT", "z1", "x1T", "s2", "g", "z2", "ctxT",
                                           "kx", "vx", "x2T", "k3", "r3", "v3")])
        s_filled = [sem(f"s_filled{c}") for c in range(6)]
        t_filled = [sem(f"t_filled{c}") for c in range(6)]
        o_filled = [sem(f"o_filled{c}") for c in range(2)]
        exp_done = [sem(f"exp_done{c}") for c in range(6)]
        a_ = sems("xT_ready", "q_hi", "k_hi", "v_hi", "v_mid", "yT_ready", "x1T_ready", "a_exp_done", "g_ready",
                  "vx_ready", "x2T_ready", "k_relu_done", "r_tanh_done")
        max_done = [sem(f"max_done{c}") for c in range(6)]
        p_hi_done = [sem(f"p_hi_done{c}") for c in range(6)]
        o_summed = [sem(f"o_summed{c}") for c in range(2)]
        o_inverse = [sem(f"o_inverse{c}") for c in range(2)]
        y_ready = [sem(f"y_ready{c}") for c in range(2)]
        v_ = sems("q_lo", "k_lo", "v_rest_done", "shift_done", "shift_hi", "shift_lo", "kxT_ready", "ctxT_ready",
                  "s2_max_done", "s2_neg_done", "s2_rec_done", "a_ready", "sum1_done", "sum2_done", "sum3_done",
                  "gated_done", "xr_ready", "xk_ready", "x1_ready", "x2_ready", "x3_ready")
        bn_done = [sem(f"bn_done{i}") for i in range(3)]
        mv_done = [sem(f"mv_done{i}") for i in range(3)]
        p_lo_done = [sem(f"p_lo_done{c}") for c in range(6)]
        g_ = sems("x_c_ready", "x1p_ready", "v_lo", "dx_done", "k_act_ready")
        var_done = [sem(f"var_done{i}") for i in range(3)]
        rstd_done = [sem(f"rstd_done{i}") for i in range(3)]
        x_loaded = [sem(f"x_loaded{r}") for r in range(RING)]
        parts_saved = [sem(f"parts_saved{r}") for r in range(RING)]
        stack_loaded = [sem(f"stack_loaded{r}") for r in range(RING)]
        shift_loaded = [sem(f"shift_loaded{r}") for r in range(RING)]
        ctx_loaded = sem("ctx_loaded")
        x_res_loaded = sem("x_res_loaded")
        out_saved = sem("out_saved")
        raw_loaded = {n: sem("raw_loaded_" + n) for n in raw_names}
        lsr_loaded = sem("lsr_loaded")
        small_loaded = sem("small_loaded")
        consts_ready = sem("consts_ready")
        consts_step = sem("consts_step")
        dve_consts = sem("dve_consts")
        setup_filled = sem("setup_filled")
        setup_taken = sem("setup_taken")

        def wait(eng, s, count):
            if not isinstance(count, int) or count > 0:
                eng.wait_ge(s, count)

        BANK_USERS = [
            [("yT", CROSS, a_["yT_ready"]), ("z1", CROSS, v_["sum1_done"]), ("x2T", FFN, a_["x2T_ready"]),
             ("v", SCORES, v_["v_rest_done"]), ("k3", FFN, a_["k_relu_done"]), ("r3", FFN, a_["r_tanh_done"]),
             ("v3", FFN, v_["gated_done"]), ("g", CROSS, a_["g_ready"]), ("z2", CROSS, v_["sum2_done"])],
            [("xT", IN, a_["xT_ready"]), ("q", IN, v_["q_lo"]), ("k", IN, v_["k_lo"]), ("x1T", CROSS, a_["x1T_ready"]),
             ("s2", CROSS, a_["a_exp_done"]), ("ctxT", PROBS, v_["ctxT_ready"]), ("mT", SCORES, v_["shift_done"]),
             ("kx", PROBS, v_["kxT_ready"]), ("vx", PROBS, a_["vx_ready"])],
        ]
        WHERE = {u[0]: (bank, i) for bank in range(2) for i, u in enumerate(BANK_USERS[bank])}

        def bank_free(pe, what, turn, at):
            bank, i = WHERE[what]
            users = BANK_USERS[bank]
            for back in range(1, 3 * len(users)):
                j = (i - back) % len(users)
                _, skew, read = users[j]
                at_j = at + (i - back - j) // len(users)
                b = Batch(turn, at_j, skew)
                if not b.static or 0 <= b.n < B:
                    pe.wait_ge(read, b.n + 1)
                    break
            else:
                pe.wait_ge(setup_taken, SETUP_TOTAL)
            return ps_m[bank]

        NARROW, WIDE = (0, 1), (2, 3, 4, 5)
        S_ORDER = [0, 2, 1, 3, 4, 5]
        T_ORDER = [0, 2, 3, 1, 4, 5]

        def chunk_heads(c):
            return range(8 * c, 8 * c + 8) if c in NARROW else range(4 * (c - 2), 4 * (c - 2) + 4)

        def column(c, h):
            width = P if c in NARROW else T
            return 512 * (h % 2) + width * ((h - chunk_heads(c)[0]) // 2)

        def before(order, c, b):
            i = order.index(c)
            return (order[i - 1], b.n + 1) if i else (order[-1], b.n)

        block = es.enter_context(nc.Block())

        def live(turn, at, skew):
            b = Batch(turn, at, skew)
            return not b.static or 0 <= b.n < B

        def run_steps(eng, step, ahead=0):
            first = LAST_SKEW + 1
            loops = (B - first) // RING
            for t in range(first):
                step(t // RING, t % RING)
            q0, r0 = first // RING, first % RING
            with eng.Fori(q0, q0 + loops) as q:
                for u in range(RING):
                    step(q, r0 + u)
            for t in range(first + loops * RING, B + LAST_SKEW + ahead):
                step(t // RING, t % RING)

        @block.sync
        def _(sp):
            sp.dma_start(lsr[:, 0], Wq_lsr.rearrange("(a h) d r -> (h d) a r", a=KC)).then_inc(lsr_loaded, 16)
            sp.dma_start(lsr[:, 1], Wk_lsr.rearrange("(a h) d r -> (h d) a r", a=KC)).then_inc(lsr_loaded, 16)
            for n in raw_names:
                sp.dma_start(raw[n], raw_dram[n].rearrange("(a p) c -> p a c", p=P)).then_inc(raw_loaded[n], 16)
            for i, v in enumerate((bq, bk, bv, mu_r, mu_k)):
                with nc.allow_non_contiguous_dma(reason="256 values to a column each"):
                    sp.dma_start(cols[:, i, :], v.rearrange("(a p) -> p a", p=P)).then_inc(small_loaded, 16)
            for i, v in enumerate((bo, proj_b)):
                sp.dma_start(rows[:, i, :], v.rearrange("(o c) -> o c", o=1)).then_inc(small_loaded, 16)
            sp.dma_start(mask_i[:], mask_in.rearrange("(m o) -> m o", o=1)).then_inc(small_loaded, 16)
            sp.wait_ge(consts_ready, 1)

            def tokens(ap, n):
                return ap[n, :, :] if isinstance(n, int) else ap[bass.ds(n, 1), :, :].rearrange("o t c -> (o t) c")

            def load_x(b):
                wait(sp, filled["f_xT"], b.n - 2)
                sp.dma_start(x_in[b.slot][:], tokens(x, b.n).rearrange("(j p) c -> p j c", p=P)) \
                    .then_inc(x_loaded[b.slot], 16)

            def step(turn, at):
                if live(turn, at, IN):
                    load_x(Batch(turn, at, IN))
                at = at - 1
                b = Batch(turn, at, IN)
                if live(turn, at, SCORES):
                    c = Batch(turn, at, SCORES)
                    wait(sp, filled["f_ctxT"], c.n)
                    sp.dma_start(ctx_sb[:], tokens(ctx_in, c.n)).then_inc(ctx_loaded, 16)
                if live(turn, at, PROBS):
                    c = Batch(turn, at, PROBS)
                    wait(sp, g_["x_c_ready"], c.n)
                    sp.dma_start(x_res[:], tokens(x, c.n).rearrange("(j p) c -> p j c", p=P)).then_inc(x_res_loaded, 16)
                if live(turn, at, IN):
                    for s, ready in enumerate(("q_lo", "k_lo")):
                        sp.wait_ge(v_[ready], b.n + 1)
                        sp.dma_start(parts_dram[s][b.slot].rearrange("(a p) w t -> p a w t", p=P), parts[s][:].bitcast(F32)) \
                            .then_inc(parts_saved[b.slot], 16)
                    sp.wait_ge(parts_saved[b.slot], b.dma_count(2))
                    wait(sp, t_filled[T_ORDER[-1]], b.n - 2)
                    for s, which in enumerate(((0, 0, 1), (0, 1, 0))):
                        for g in range(2):
                            for row, part in enumerate(which):
                                src = parts_dram[s][b.slot].rearrange("(j g d) w t -> g w d j t", g=2, d=DH)[g, part]
                                r0 = 64 * g + DH * row
                                sp.dma_start(stack[s][b.slot][r0:r0 + DH].bitcast(F32), src).then_inc(stack_loaded[b.slot], 16)
                if live(turn, at, SCORES):
                    c = Batch(turn, at, SCORES)
                    sp.wait_ge(v_["shift_lo"], c.n + 1)
                    for g in range(2):
                        for part in range(2):
                            r0 = 64 * g + ONES_ROW + part
                            sp.dma_start(stack[0][c.slot][r0:r0 + 1].bitcast(F32),
                                         shift_parts[8 * g:8 * g + 8, part, :].bitcast(F32)).then_inc(shift_loaded[c.slot], 16)
                if live(turn, at, FFN):
                    c = Batch(turn, at, FFN)
                    sp.wait_ge(v_["x3_ready"], c.n + 1)
                    sp.dma_start(tokens(out, c.n).rearrange("(j p) c -> p j c", p=P), x3[:]).then_inc(out_saved, 16)

            run_steps(sp, step, ahead=1)
            sp.wait_ge(out_saved, 16 * B)

        @block.tensor
        def _(pe):
            bank_no = [0]

            def setup_bank():
                n = bank_no[0]
                bank_no[0] += 1
                if n >= 2:
                    pe.wait_ge(setup_taken, n - 1)
                return ps_m[n % 2]

            pe.wait_ge(consts_ready, 1)
            pe.wait_ge(lsr_loaded, 32)
            bank = setup_bank()
            for s in range(2):
                for a in range(KC):
                    i = s * KC + a
                    last = nc.tensor.transpose(bank[0:RANK, i * P:(i + 1) * P], lsr[:, s, a, :], ident[:])
            last.then_inc(setup_filled, 1)
            bank = setup_bank()
            pe.wait_ge(setup_taken, 1)
            for a in range(KC):
                last = nc.tensor.matmul(bank[:, a * P:(a + 1) * P], lsrT[:, 0, a, :], lsrT[:, 1, a, :],
                                        start=True, stop=True)
            last.then_inc(setup_filled, 1)
            pe.wait_ge(raw_loaded["Wq"], 16)
            pe.wait_ge(setup_taken, 2)
            pe.wait_ge(small_loaded, 16 * 8)
            for k in range(KC):
                bank = setup_bank()
                for a in range(KC):
                    last = nc.tensor.matmul(bank[:, a * P:(a + 1) * P], raw["Wq"][:, a, k * P:(k + 1) * P],
                                            lsr_prod[:, a, :], start=True, stop=True)
                last.then_inc(setup_filled, 1)
            bank = setup_bank()
            for a in range(KC):
                last = nc.tensor.matmul(bank[:, a:a + 1], lsr_prod[:, a, :], cols[:, BQ, a:a + 1], start=True, stop=True)
            last.then_inc(setup_filled, 1)
            for n in turned_names:
                pe.wait_ge(raw_loaded[n], 16)
                for k in range(KC):
                    bank = setup_bank()
                    for a in range(KC):
                        last = nc.tensor.transpose(bank[:, a * P:(a + 1) * P], raw[n][:, a, k * P:(k + 1) * P], ident[:])
                    last.then_inc(setup_filled, 1)
            for n in ("Wxq", "Wxk"):
                pe.wait_ge(raw_loaded[n], 16)
            for k in range(KC):
                bank = setup_bank()
                for a in range(KC):
                    last = nc.tensor.matmul(bank[:, 0:C], raw["Wxk"][:, a, k * P:(k + 1) * P], raw["Wxq"][:, a, :],
                                            start=(a == 0), stop=(a == KC - 1))
                last.then_inc(setup_filled, 1)
            bank = setup_bank()
            pe.wait_ge(dve_consts, 1)
            pe.wait_ge(setup_taken, 5 + 2 * (turned_names.index("Wo") + 1))
            for a in range(KC):
                nc.tensor.matmul(bank[:, 0:C], bv_rep[:, a, :], wT["Wo"][:, a, :], start=(a == 0), stop=False)
            nc.tensor.matmul(bank[:, 0:C], ones_row[:], rows[:, 0, :], start=False, stop=True).then_inc(setup_filled, 1)
            bank = setup_bank()
            nc.tensor.matmul(bank[:, 0:C], ones_row[:], rows[:, 1, :], start=True, stop=True).then_inc(setup_filled, 1)
            assert bank_no[0] == SETUP_TOTAL
            pe.wait_ge(setup_taken, SETUP_TOTAL)

            def turn_tiles(bank, src):
                for k in range(KC):
                    for j in range(NT):
                        last = nc.tensor.transpose(bank[:, k * T + j * P:k * T + (j + 1) * P],
                                                   src[:, j, k * P:(k + 1) * P], ident[:])
                return last

            def rows_out(bank, w, src):
                n = src.shape[-1]
                for a in range(KC):
                    for k in range(KC):
                        last = nc.tensor.matmul(bank[:, a * n:(a + 1) * n], w[:, k, a * P:(a + 1) * P], src[:, k, :],
                                                start=(k == 0), stop=(k == KC - 1))
                return last

            def tokens_out(bank, src, w, tiles=NT, rows=P):
                for j in range(tiles):
                    for k in range(KC):
                        last = nc.tensor.matmul(bank[0:rows, j * C:(j + 1) * C], src[:, k, j * P:j * P + rows], w[:, k, :],
                                                start=(k == 0), stop=(k == KC - 1))
                return last

            def scores(b, c, target, free, free_count, done, left, right, mask):
                wait(pe, free, free_count)
                heads = chunk_heads(c)
                rows_at = 0 if (c in NARROW) == (left is stack[0]) else P
                width, col = (P, rows_at) if c in NARROW else (T, 0)
                for h in heads:
                    r0 = 64 * (h % 2)
                    at_h = column(c, h)
                    o = target[:, at_h:at_h + width]
                    first_in_bank = h - heads[0] < 2
                    rows_n = STACK_ROWS if left is stack[1] else ONES_ROW
                    nc.tensor.matmul(o, left[b.slot][r0:r0 + rows_n, h // 2, rows_at:rows_at + P],
                                     right[b.slot][r0:r0 + rows_n, h // 2, col:col + width],
                                     start=first_in_bank, stop=False, skip_group_check=True)
                for half in range(2):
                    o = target[:, half * 512:(half + 1) * 512]
                    if c in NARROW:
                        last = nc.tensor.matmul(o, identb[:], mask[:].rearrange("p a b -> p (a b)"),
                                                start=False, stop=True, skip_group_check=True)
                    else:
                        o = o.rearrange("p (n w) -> p n w", n=2)
                        o = o[:, :, P:2 * P] if left is stack[0] else o[:, :, 0:P]
                        last = nc.tensor.matmul(o, identb[:], mask[:, 0:2, :], start=False, stop=True,
                                                skip_group_check=True)
                last.then_inc(done, 1)

            def step(turn, at):
                A, Sb, Pb, X, F = (Batch(turn, at, s) for s in range(5))
                on = [live(turn, at, s) for s in range(5)]

                def S(c):
                    if on[SCORES]:
                        if c == S_ORDER[0]:
                            pe.wait_ge(stack_loaded[Sb.slot], Sb.dma_count(12))
                        prev, count = before(S_ORDER, c, Sb)
                        scores(Sb, c, ps_s, max_done[prev], count, s_filled[c], stack[0], stack[1], mask_s)

                def Tr(c):
                    if on[PROBS]:
                        if c == T_ORDER[0]:
                            pe.wait_ge(shift_loaded[Pb.slot], Pb.dma_count(4))
                        prev, count = before(T_ORDER, c, Pb)
                        scores(Pb, c, ps_t, exp_done[prev], count, t_filled[c], stack[1], stack[0], mask_t)

                def PV(half):
                    if not on[PROBS]:
                        return
                    b = Pb
                    wait(pe, o_summed[1 - half], 2 * (b.n + half))
                    if half == 0:
                        pe.wait_ge(g_["v_lo"], b.n + 1)
                    for c in (half, 2 + 2 * half, 3 + 2 * half):
                        pe.wait_ge(p_lo_done[c], b.n + 1)
                    for h8 in range(8):
                        h = 8 * half + h8
                        w = 2 + h // 4
                        cw, cn = column(w, h), column(half, h)
                        v = [v_parts[b.slot][:, j, h].rearrange("p a d -> p (a d)") for j in range(2)]
                        n = v[0].shape[-1]
                        for i in range(NT):
                            o = ps_o[:, i, h8 * n:(h8 + 1) * n]
                            terms = [(p[w][:, cw + i * P:cw + (i + 1) * P], v[0]) for p in (p_hi, p_lo)]
                            if i == 1:
                                terms += [(p[half][:, cn:cn + P], v[1]) for p in (p_hi, p_lo)]
                            for e, (p, vv) in enumerate(terms):
                                last = nc.tensor.matmul(o, p, vv, start=(e == 0), stop=(e == len(terms) - 1),
                                                        skip_group_check=True)
                    last.then_inc(o_filled[half], 1)

                if on[CROSS]:
                    bank = bank_free(pe, "yT", turn, at)
                    pe.wait_ge(y_ready[1], X.n + 1)
                    turn_tiles(bank, y[:].rearrange("p j h d -> p j (h d)")).then_inc(filled["f_yT"], 1)
                S(0)
                if on[IN]:
                    bank = bank_free(pe, "xT", turn, at)
                    pe.wait_ge(x_loaded[A.slot], A.dma_count(1))
                    turn_tiles(bank, x_in[A.slot]).then_inc(filled["f_xT"], 1)
                Tr(0)
                if on[CROSS]:
                    bank = bank_free(pe, "z1", turn, at)
                    tokens_out(bank, yT, wT["Wo"]).then_inc(filled["f_z1"], 1)
                S(2)
                if on[IN]:
                    bank = bank_free(pe, "q", turn, at)
                    rows_out(bank, wq_fold, xT[A.slot]).then_inc(filled["f_q"], 1)
                Tr(2)
                if on[FFN]:
                    bank = bank_free(pe, "x2T", turn, at)
                    pe.wait_ge(v_["x2_ready"], F.n + 1)
                    turn_tiles(bank, x2[F.slot]).then_inc(filled["f_x2T"], 1)
                S(1)
                if on[IN]:
                    bank = bank_free(pe, "k", turn, at)
                    rows_out(bank, wT["Wk"], xT[A.slot]).then_inc(filled["f_k"], 1)
                Tr(3)
                if on[SCORES]:
                    bank = bank_free(pe, "v", turn, at)
                    tokens_out(bank, xT[Sb.slot], wT["Wv"]).then_inc(filled["f_v"], 1)
                S(3)
                Tr(1)
                if on[CROSS]:
                    bank = bank_free(pe, "x1T", turn, at)
                    pe.wait_ge(v_["x1_ready"], X.n + 1)
                    turn_tiles(bank, x1).then_inc(filled["f_x1T"], 1)
                S(4)
                if on[FFN]:
                    bank = bank_free(pe, "k3", turn, at)
                    pe.wait_ge(v_["xk_ready"], F.n + 1)
                    rows_out(bank, wT["Wkf"], xk).then_inc(filled["f_k3"], 1)
                PV(0)
                if on[CROSS]:
                    bank = bank_free(pe, "s2", turn, at)
                    for j in range(NT):
                        for k in range(KC):
                            last = nc.tensor.matmul(bank[:, j * M:(j + 1) * M], x1T[:, k, j * P:(j + 1) * P],
                                                    kxT[X.slot][:, k, :], start=(k == 0), stop=(k == KC - 1))
                    last.then_inc(filled["f_s2"], 1)
                S(5)
                if on[FFN]:
                    bank = bank_free(pe, "r3", turn, at)
                    pe.wait_ge(v_["xr_ready"], F.n + 1)
                    tokens_out(bank, xr, wT["Wr"]).then_inc(filled["f_r3"], 1)
                Tr(4)
                if on[PROBS]:
                    bank = bank_free(pe, "ctxT", turn, at)
                    pe.wait_ge(ctx_loaded, (Pb.n + 1) * 16)
                    for k in range(KC):
                        last = nc.tensor.transpose(bank[:, k * M:(k + 1) * M], ctx_sb[:, k * P:(k + 1) * P],
                                                   ident[0:M, 0:M])
                    last.then_inc(filled["f_ctxT"], 1)
                if on[FFN]:
                    bank = bank_free(pe, "v3", turn, at)
                    pe.wait_ge(g_["k_act_ready"], F.n + 1)
                    tokens_out(bank, k_act, wT["Wvf"]).then_inc(filled["f_v3"], 1)
                if on[SCORES]:
                    bank = bank_free(pe, "mT", turn, at)
                    pe.wait_ge(max_done[5], Sb.n + 1)
                    for i in range(NT):
                        last = nc.tensor.transpose(bank[0:HEADS, i * P:(i + 1) * P],
                                                   row_max[:, i].rearrange("p g j -> p (g j)"), ident[:])
                    last.then_inc(filled["f_mT"], 1)
                Tr(5)
                if on[CROSS]:
                    bank = bank_free(pe, "g", turn, at)
                    pe.wait_ge(v_["a_ready"], X.n + 1)
                    for k in range(KC):
                        last = nc.tensor.matmul(bank[0:M, 0:C], a_nrm[:, k, :], wT["Wp"][:, k, :],
                                                start=(k == 0), stop=(k == KC - 1))
                    last.then_inc(filled["f_g"], 1)
                if on[PROBS]:
                    bank = bank_free(pe, "kx", turn, at)
                    pe.wait_ge(v_["ctxT_ready"], Pb.n + 1)
                    rows_out(bank, wx_fold, ctxT).then_inc(filled["f_kx"], 1)
                PV(1)
                if on[CROSS]:
                    bank = bank_free(pe, "z2", turn, at)
                    for j in range(NT):
                        last = nc.tensor.matmul(bank[:, j * C:(j + 1) * C], vx[X.slot][:, j * P:(j + 1) * P], g_sb[:],
                                                start=True, stop=True)
                    last.then_inc(filled["f_z2"], 1)
                if on[PROBS]:
                    bank = bank_free(pe, "vx", turn, at)
                    tokens_out(bank, ctxT, wT["Wxv"], tiles=1, rows=M).then_inc(filled["f_vx"], 1)

            run_steps(pe, step)

        @block.scalar
        def _(act):
            def flat(t):
                return t[:].rearrange("p a b -> p (a b)")

            def step(turn, at):
                A, Sb, Pb, X, F = (Batch(turn, at, s) for s in range(5))
                on = [live(turn, at, s) for s in range(5)]

                def exp(c):
                    if not on[PROBS]:
                        return
                    i = T_ORDER.index(c)
                    act.wait_ge(t_filled[c], Pb.n + 1)
                    prev, count = (T_ORDER[i - 3], Pb.n + 1) if i >= 3 else (T_ORDER[i + 3], Pb.n)
                    wait(act, p_lo_done[prev], count)
                    nc.scalar.activation(p32[i % 3][:], ps_t[:], ACT.Exp).then_inc(exp_done[c], 1)

                def split_hi(b, s, name, bias, what):
                    act.wait_ge(filled["f_" + what], b.n + 1)
                    prev = Batch(turn, at - 1, IN)
                    if not prev.static or prev.n >= 0:
                        act.wait_ge(parts_saved[prev.slot], prev.dma_count(2))
                    bank = ps_m[WHERE[what][0]]
                    for a in range(KC):
                        last = nc.scalar.activation(parts[s][:, a, 0, :], bank[:, a * T:(a + 1) * T], ACT.Identity,
                                                    bias=bias[a])
                    last.then_inc(a_[name], 1)

                if on[CROSS]:
                    act.wait_ge(filled["f_yT"], X.n + 1)
                    wait(act, filled["f_z1"], X.n)
                    nc.scalar.copy(flat(yT), ps_m[0][:]).then_inc(a_["yT_ready"], 1)
                if on[IN]:
                    act.wait_ge(filled["f_xT"], A.n + 1)
                    wait(act, filled["f_v"], A.n - 2)
                    nc.scalar.copy(flat(xT[A.slot]), ps_m[1][:]).then_inc(a_["xT_ready"], 1)
                exp(0)
                if on[IN]:
                    split_hi(A, 0, "q_hi", [bq_fold[:, a:a + 1] for a in range(KC)], "q")
                exp(2)
                if on[FFN]:
                    act.wait_ge(filled["f_x2T"], F.n + 1)
                    wait(act, v_["xk_ready"], F.n)
                    nc.scalar.copy(x2T[:, :, 1:1 + T], ps_m[0][:].rearrange("p (a b) -> p a b", a=KC)) \
                        .then_inc(a_["x2T_ready"], 1)
                if on[IN]:
                    split_hi(A, 1, "k_hi", [cols[:, BK, a:a + 1] for a in range(KC)], "k")
                exp(3)
                if on[SCORES]:
                    act.wait_ge(filled["f_v"], Sb.n + 1)
                    wait(act, o_filled[1], Sb.n - 2)
                    for j in range(NT):
                        last = nc.scalar.copy(v_parts[Sb.slot][:, j, :, 0, 0:DH],
                                              ps_m[0][:, j * C:(j + 1) * C].rearrange("p (h d) -> p h d", h=HEADS))
                    last.then_inc(a_["v_hi"], 1)
                exp(1)
                if on[SCORES]:
                    act.wait_ge(v_["v_rest_done"], Sb.n + 1)
                    for j in range(NT):
                        last = nc.scalar.copy(v_parts[Sb.slot][:, j, :, 1, 0:DH],
                                              v_rest[:, j, :].rearrange("p (h d) -> p h d", h=HEADS))
                    last.then_inc(a_["v_mid"], 1)
                if on[CROSS]:
                    act.wait_ge(filled["f_x1T"], X.n + 1)
                    wait(act, filled["f_s2"], X.n)
                    nc.scalar.copy(flat(x1T), ps_m[1][:]).then_inc(a_["x1T_ready"], 1)
                if on[FFN]:
                    act.wait_ge(filled["f_k3"], F.n + 1)
                    wait(act, g_["k_act_ready"], F.n)
                    nc.scalar.activation(flat(k_relu), ps_m[0][:], ACT.Relu).then_inc(a_["k_relu_done"], 1)
                if on[CROSS]:
                    act.wait_ge(v_["s2_neg_done"], X.n + 1)
                    wait(act, v_["a_ready"], X.n)
                    for j in range(NT):
                        last = nc.scalar.activation(a_exp[:, j, :], ps_m[1][:, j * M:(j + 1) * M], ACT.Exp,
                                                    bias=s2_neg[:, j:j + 1], scale=XSCALE, accum_out=s2_sum[:, j:j + 1])
                    last.then_inc(a_["a_exp_done"], 1)
                if on[FFN]:
                    act.wait_ge(filled["f_r3"], F.n + 1)
                    wait(act, v_["gated_done"], F.n)
                    nc.scalar.activation(flat(r_tanh), ps_m[0][:], ACT.Tanh, scale=0.5).then_inc(a_["r_tanh_done"], 1)
                exp(4)
                exp(5)
                if on[CROSS]:
                    act.wait_ge(filled["f_g"], X.n + 1)
                    wait(act, filled["f_z2"], X.n)
                    nc.scalar.activation(g_sb[:], ps_m[0][0:M, 0:C], ACT.Copy, scale=keep[:]) \
                        .then_inc(a_["g_ready"], 1)
                if on[PROBS]:
                    act.wait_ge(filled["f_vx"], Pb.n + 1)
                    wait(act, filled["f_z2"], Pb.n - 2)
                    nc.scalar.copy(vx[Pb.slot][:], ps_m[1][0:M, 0:C]).then_inc(a_["vx_ready"], 1)

            act.wait_ge(setup_taken, SETUP_TOTAL)
            run_steps(act, step)

        @block.vector
        def _(dve):
            taken = [0]

            def setup_take(count=1):
                n = taken[0]
                dve.wait_ge(setup_filled, n + 1)
                taken[0] += 1
                return ps_m[n % 2]

            def copy_bank(dst, width=C):
                bank = setup_take()
                nc.vector.tensor_copy(dst, bank[:, 0:width]).then_inc(setup_taken, 1)

            dve.wait_ge(consts_ready, 1)
            dve.wait_ge(small_loaded, 16 * 8)
            nc.vector.tensor_scalar(keep[:], mask_i[:], 0.0, None, ALU.not_equal)
            for a in range(KC):
                last = nc.vector.tensor_scalar(bv_rep[:, a, :], ident[:], 0.0, cols[:, BV, a:a + 1], ALU.mult, ALU.add)
            last.then_inc(dve_consts, 1)
            bank = setup_take()
            nc.vector.tensor_copy(lsrT[:].rearrange("r s a p -> r (s a p)"), bank[0:RANK, :]).then_inc(setup_taken, 1)
            bank = setup_take()
            for a in range(KC):
                last = nc.vector.scalar_tensor_tensor(lsr_prod[:, a, :], bank[:, a * P:(a + 1) * P], float(RANK) ** -0.5,
                                                      block_diag[:], op0=ALU.mult, op1=ALU.mult)
            last.then_inc(setup_taken, 1)
            for k in range(KC):
                copy_bank(wq_fold[:, k, :])
            copy_bank(bq_fold[:], KC)
            for n in turned_names:
                for k in range(KC):
                    copy_bank(wT[n][:, k, :])
            for k in range(KC):
                copy_bank(wx_fold[:, k, :])
            copy_bank(c1[:])
            copy_bank(pb_rep[:])
            assert taken[0] == SETUP_TOTAL
            dve.wait_ge(setup_taken, SETUP_TOTAL)

            def step(turn, at):
                A, Sb, Pb, X, F = (Batch(turn, at, s) for s in range(5))
                on = [live(turn, at, s) for s in range(5)]

                def row_maxima(c):
                    if not on[SCORES]:
                        return
                    dve.wait_ge(s_filled[c], Sb.n + 1)
                    if c == S_ORDER[0]:
                        wait(dve, filled["f_mT"], Sb.n)
                    heads = chunk_heads(c)
                    tile = 0 if c in NARROW else 1
                    j0, nj = heads[0] // 2, len(heads) // 2
                    nc.vector.tensor_reduce(row_max[:, tile, :, j0:j0 + nj],
                                            ps_s[:].rearrange("p (g j w) -> p g j w", j=nj, g=2), AX_X, ALU.max) \
                        .then_inc(max_done[c], 1)

                def high_part(c):
                    if not on[PROBS]:
                        return
                    dve.wait_ge(exp_done[c], Pb.n + 1)
                    half = c if c in NARROW else (c - 2) // 2
                    wait(dve, o_filled[half], Pb.n)
                    nc.vector.tensor_copy(p_hi[c][:], p32[T_ORDER.index(c) % 3][:]).then_inc(p_hi_done[c], 1)

                def split_lo(b, s, hi, lo, bias, what):
                    dve.wait_ge(a_[hi], b.n + 1)
                    bank = ps_m[WHERE[what][0]]
                    for a in range(KC):
                        last = nc.vector.scalar_tensor_tensor(parts[s][:, a, 1, :], bank[:, a * T:(a + 1) * T], bias[a],
                                                              parts[s][:, a, 0, :].bitcast(F32),
                                                              op0=ALU.add, op1=ALU.subtract)
                    last.then_inc(v_[lo], 1)

                def stats(i, b, src, summed):
                    dve.wait_ge(summed, b.n + 1)
                    wait(dve, mv_done[i], b.n)
                    for j in range(NT):
                        last = nc.vector.bn_stats(bn[i][:, j, :], src[:, j, :])
                    last.then_inc(bn_done[i], 1)
                    dve.wait_ge(bn_done[i], b.n + 1)
                    wait(dve, rstd_done[i], b.n)
                    nc.vector.memset(pause[:], 0.0)
                    for j in range(NT):
                        last = nc.vector.bn_aggr(mv[i][:, j, :], bn[i][:, j, :])
                    last.then_inc(mv_done[i], 1)

                def normalise(i, b, dst, src, done):
                    dve.wait_ge(rstd_done[i], b.n + 1)
                    for j in range(NT):
                        last = nc.vector.tensor_scalar(dst[:, j, :], src[:, j, :], mv[i][:, j, 0:1], rstd[i][:, j:j + 1],
                                                       ALU.subtract, ALU.mult)
                    last.then_inc(v_[done], 1)

                def attention_out(half):
                    if not on[PROBS]:
                        return
                    b = Pb
                    dve.wait_ge(o_filled[half], b.n + 1)
                    wait(dve, y_ready[1 - half], b.n + half)
                    for i in range(NT):
                        nc.vector.tensor_reduce(o_sum[:, i],
                                                ps_o[:, i, 0:8 * 3 * (DH + 1)].rearrange("p (h a d) -> p h d a", h=8, a=3),
                                                AX_X, ALU.add).then_inc(o_summed[half], 1)
                    dve.wait_ge(o_summed[half], (b.n + 1) * 2)
                    nc.vector.reciprocal(o_rec[:], o_sum[:, :, :, DH]).then_inc(o_inverse[half], 1)
                    dve.wait_ge(o_inverse[half], b.n + 1)
                    wait(dve, filled["f_yT"], b.n)
                    for i in range(NT):
                        last = nc.vector.tensor_tensor(y[:, i, 8 * half:8 * half + 8, :], o_sum[:, i, :, 0:DH],
                                                       o_rec[:, i, :].unsqueeze(2).to_broadcast([P, 8, DH]), ALU.mult)
                    last.then_inc(y_ready[half], 1)

                row_maxima(0)
                high_part(0)
                if on[CROSS]:
                    dve.wait_ge(filled["f_z1"], X.n + 1)
                    dve.wait_ge(g_["x_c_ready"], X.n + 1)
                    wait(dve, v_["x1_ready"], X.n)
                    nc.vector.tensor_tensor(sum1[:].rearrange("p a b -> p (a b)"), ps_m[0][:],
                                            x_c[:].rearrange("p a b -> p (a b)"), ALU.add).then_inc(v_["sum1_done"], 1)
                    stats(0, X, sum1, v_["sum1_done"])
                row_maxima(2)
                if on[IN]:
                    split_lo(A, 0, "q_hi", "q_lo", [bq_fold[:, a:a + 1] for a in range(KC)], "q")
                high_part(2)
                if on[CROSS]:
                    wait(dve, filled["f_x1T"], X.n)
                    wait(dve, g_["x1p_ready"], X.n)
                    normalise(0, X, x1, sum1, "x1_ready")
                row_maxima(1)
                if on[IN]:
                    split_lo(A, 1, "k_hi", "k_lo", [cols[:, BK, a:a + 1] for a in range(KC)], "k")
                high_part(3)
                if on[FFN]:
                    dve.wait_ge(g_["dx_done"], F.n + 1)
                    for dst, mu, ready, used in ((xk, MUK, "xk_ready", "f_k3"), (xr, MUR, "xr_ready", "f_r3")):
                        wait(dve, filled[used], F.n)
                        for k in range(KC):
                            last = nc.vector.scalar_tensor_tensor(dst[:, k, :], dx[:, k, :], cols[:, mu, k:k + 1],
                                                                  x2T[:, k, 0:T], op0=ALU.mult, op1=ALU.add)
                        last.then_inc(v_[ready], 1)
                if on[SCORES]:
                    dve.wait_ge(a_["v_hi"], Sb.n + 1)
                    wait(dve, g_["v_lo"], Sb.n)
                    for j in range(NT):
                        last = nc.vector.tensor_tensor(
                            v_rest[:, j, :].rearrange("p (h d) -> p h d", h=HEADS),
                            ps_m[0][:, j * C:(j + 1) * C].rearrange("p (h d) -> p h d", h=HEADS),
                            v_parts[Sb.slot][:, j, :, 0, 0:DH], ALU.subtract)
                    last.then_inc(v_["v_rest_done"], 1)
                row_maxima(3)
                high_part(1)
                row_maxima(4)
                if on[CROSS]:
                    dve.wait_ge(filled["f_s2"], X.n + 1)
                    wait(dve, v_["s2_neg_done"], X.n)
                    nc.vector.tensor_reduce(s2_max[:], ps_m[1][:, 0:NT * M].rearrange("p (j m) -> p j m", j=NT), AX_X,
                                            ALU.max).then_inc(v_["s2_max_done"], 1)
                    dve.wait_ge(v_["s2_max_done"], X.n + 1)
                    wait(dve, a_["a_exp_done"], X.n)
                    nc.vector.tensor_scalar(s2_neg[:], s2_max[:], -XSCALE, None, ALU.mult) \
                        .then_inc(v_["s2_neg_done"], 1)
                attention_out(0)
                row_maxima(5)
                if on[CROSS]:
                    dve.wait_ge(a_["a_exp_done"], X.n + 1)
                    wait(dve, v_["a_ready"], X.n)
                    nc.vector.reciprocal(s2_rec[:], s2_sum[:]).then_inc(v_["s2_rec_done"], 1)
                    dve.wait_ge(v_["s2_rec_done"], X.n + 1)
                    wait(dve, filled["f_g"], X.n)
                    for j in range(NT):
                        last = nc.vector.tensor_scalar(a_nrm[:, j, :], a_exp[:, j, :], s2_rec[:, j:j + 1], None, ALU.mult)
                    last.then_inc(v_["a_ready"], 1)
                high_part(4)
                if on[PROBS]:
                    dve.wait_ge(filled["f_ctxT"], Pb.n + 1)
                    wait(dve, filled["f_vx"], Pb.n)
                    nc.vector.tensor_copy(ctxT[:].rearrange("p a b -> p (a b)"), ps_m[1][:, 0:KC * M]) \
                        .then_inc(v_["ctxT_ready"], 1)
                if on[SCORES]:
                    dve.wait_ge(filled["f_mT"], Sb.n + 1)
                    wait(dve, v_["shift_lo"], Sb.n)
                    nc.vector.tensor_scalar(shift[:], ps_m[1][0:HEADS, 0:T], -1.0, LN2_12, ALU.mult, ALU.add) \
                        .then_inc(v_["shift_done"], 1)
                    dve.wait_ge(v_["shift_done"], Sb.n + 1)
                    prev = Batch(turn, at - 1, SCORES)
                    if not prev.static or prev.n >= 0:
                        dve.wait_ge(shift_loaded[prev.slot], prev.dma_count(4))
                    nc.vector.tensor_copy(shift_parts[:, 0, :], shift[:]).then_inc(v_["shift_hi"], 1)
                    dve.wait_ge(v_["shift_hi"], Sb.n + 1)
                    nc.vector.tensor_tensor(shift_parts[:, 1, :], shift[:], shift_parts[:, 0, :].bitcast(F32),
                                            ALU.subtract).then_inc(v_["shift_lo"], 1)
                if on[FFN]:
                    dve.wait_ge(filled["f_v3"], F.n + 1)
                    dve.wait_ge(a_["r_tanh_done"], F.n + 1)
                    wait(dve, v_["sum3_done"], F.n)
                    nc.vector.scalar_tensor_tensor(gated[:].rearrange("p a b -> p (a b)"),
                                                   r_tanh[:].rearrange("p a b -> p (a b)"), 1.0, ps_m[0][:],
                                                   op0=ALU.add, op1=ALU.mult).then_inc(v_["gated_done"], 1)
                    dve.wait_ge(v_["gated_done"], F.n + 1)
                    wait(dve, v_["x3_ready"], F.n)
                    nc.vector.scalar_tensor_tensor(sum3[:].rearrange("p a b -> p (a b)"),
                                                   gated[:].rearrange("p a b -> p (a b)"), 0.5,
                                                   x2[F.slot][:].rearrange("p a b -> p (a b)"),
                                                   op0=ALU.mult, op1=ALU.add).then_inc(v_["sum3_done"], 1)
                    stats(2, F, sum3, v_["sum3_done"])
                high_part(5)
                if on[PROBS]:
                    dve.wait_ge(filled["f_kx"], Pb.n + 1)
                    wait(dve, filled["f_s2"], Pb.n - 2)
                    nc.vector.tensor_copy(kxT[Pb.slot][:].rearrange("p a b -> p (a b)"), ps_m[1][:, 0:KC * M]) \
                        .then_inc(v_["kxT_ready"], 1)
                if on[FFN]:
                    wait(dve, out_saved, F.n * 16)
                    normalise(2, F, x3, sum3, "x3_ready")
                attention_out(1)
                if on[CROSS]:
                    dve.wait_ge(filled["f_z2"], X.n + 1)
                    dve.wait_ge(g_["x1p_ready"], X.n + 1)
                    wait(dve, v_["x2_ready"], X.n)
                    nc.vector.tensor_tensor(sum2[:].rearrange("p a b -> p (a b)"), ps_m[0][:],
                                            x1p[:].rearrange("p a b -> p (a b)"), ALU.add).then_inc(v_["sum2_done"], 1)
                    stats(1, X, sum2, v_["sum2_done"])
                    normalise(1, X, x2[X.slot], sum2, "x2_ready")

            run_steps(dve, step)

        @block.gpsimd
        def _(pool):
            done = [0]

            def link(ins):
                done[0] += 1
                ins.then_inc(consts_step, 1)
                pool.wait_ge(consts_step, done[0])

            g = nc.gpsimd
            link(g.memset(block_diag[:], 1.0))
            bd = block_diag[:].rearrange("p (g e) -> p g e", e=DH)
            link(g.affine_select(out=bd, in_=bd, compare_op=ALU.is_ge, fill=0.0, base=0,
                                 pattern=[[-DH, P // DH], [0, DH]], channel_multiplier=1))
            link(g.affine_select(out=bd, in_=bd, compare_op=ALU.is_ge, fill=0.0, base=DH - 1,
                                 pattern=[[DH, P // DH], [0, DH]], channel_multiplier=-1))
            link(g.memset(ident[:], 0.0))
            link(g.affine_select(out=ident[:], in_=ident[:], compare_op=ALU.not_equal, fill=1.0, base=0,
                                 pattern=[[-1, P]], channel_multiplier=1))
            link(g.tensor_copy(identb[:], ident[:]))
            link(g.memset(mask_s[:], 0.0))
            link(g.memset(mask_t[:], 0.0))
            link(g.affine_select(out=mask_s[:], in_=mask_s[:], compare_op=ALU.is_ge, fill=MASKED, base=0,
                                 pattern=[[0, 4], [-1, P]], channel_multiplier=1))
            link(g.affine_select(out=mask_t[:], in_=mask_t[:], compare_op=ALU.is_ge, fill=MASKED, base=0,
                                 pattern=[[0, 4], [1, P]], channel_multiplier=-1))
            link(g.memset(ones_row[:], 1.0))
            link(g.memset(neg_half[:], -0.5))
            link(g.memset(eps[:], EPS))
            link(g.memset(x2T[:, :, 0:1], 0.0))
            for r in range(RING):
                for h in range(2):
                    link(g.memset(stack[1][r][64 * h + 32:64 * h + 64].bitcast(F32), 1.0))
                link(g.memset(v_parts[r][:], 0.0))
                link(g.memset(v_parts[r][:, :, :, 0, DH:DH + 1], 1.0))
            g.memset(mv[0][:], 0.0).then_inc(consts_ready, 1)
            pool.wait_ge(setup_taken, SETUP_TOTAL)

            def low_part(c, b):
                pool.wait_ge(p_hi_done[c], b.n + 1)
                i = T_ORDER.index(c)
                g.tensor_tensor(p_lo[c][:], p32[i % 3][:], p_hi[c][:], ALU.subtract).then_inc(p_lo_done[c], 1)

            def inverse_deviation(i, b):
                pool.wait_ge(mv_done[i], b.n + 1)
                g.tensor_tensor(var[i][:], mv[i][:, :, 1], eps[:], ALU.add).then_inc(var_done[i], 1)
                pool.wait_ge(var_done[i], b.n + 1)
                g.tensor_tensor(rstd[i][:], var[i][:], neg_half[:], ALU.pow).then_inc(rstd_done[i], 1)

            def step(turn, at):
                A, Sb, Pb, X, F = (Batch(turn, at, s) for s in range(5))
                on = [live(turn, at, s) for s in range(5)]
                if on[CROSS]:
                    pool.wait_ge(x_res_loaded, (X.n + 1) * 16)
                    wait(pool, v_["sum1_done"], X.n)
                    g.tensor_tensor(x_c[:], x_res[:], c1[:].unsqueeze(1).to_broadcast([P, NT, C]), ALU.add) \
                        .then_inc(g_["x_c_ready"], 1)
                if on[PROBS]:
                    low_part(0, Pb)
                if on[CROSS]:
                    inverse_deviation(0, X)
                if on[PROBS]:
                    low_part(2, Pb)
                if on[FFN]:
                    pool.wait_ge(a_["x2T_ready"], F.n + 1)
                    wait(pool, v_["xr_ready"], F.n)
                    g.tensor_tensor(dx[:], x2T[:, :, 1:1 + T], x2T[:, :, 0:T], ALU.subtract) \
                        .then_inc(g_["dx_done"], 1)
                if on[PROBS]:
                    low_part(3, Pb)
                if on[CROSS]:
                    pool.wait_ge(v_["x1_ready"], X.n + 1)
                    wait(pool, v_["sum2_done"], X.n)
                    g.tensor_tensor(x1p[:], x1[:], pb_rep[:].unsqueeze(1).to_broadcast([P, NT, C]), ALU.add) \
                        .then_inc(g_["x1p_ready"], 1)
                if on[PROBS]:
                    low_part(1, Pb)
                if on[SCORES]:
                    pool.wait_ge(a_["v_mid"], Sb.n + 1)
                    for j in range(NT):
                        last = g.tensor_tensor(v_parts[Sb.slot][:, j, :, 2, 0:DH],
                                               v_rest[:, j, :].rearrange("p (h d) -> p h d", h=HEADS),
                                               v_parts[Sb.slot][:, j, :, 1, 0:DH], ALU.subtract)
                    last.then_inc(g_["v_lo"], 1)
                if on[FFN]:
                    pool.wait_ge(a_["k_relu_done"], F.n + 1)
                    wait(pool, filled["f_v3"], F.n)
                    g.tensor_tensor(k_act[:], k_relu[:], k_relu[:], ALU.mult).then_inc(g_["k_act_ready"], 1)
                if on[PROBS]:
                    low_part(4, Pb)
                if on[FFN]:
                    inverse_deviation(2, F)
                if on[PROBS]:
                    low_part(5, Pb)
                if on[CROSS]:
                    inverse_deviation(1, X)

            run_steps(pool, step)


SETUP_TOTAL = 5 + 2 * 8 + 2 + 2


_INS = ['x', 'ctx_1024', 'mask_S2_ik0', 'L0_attn_Wq', 'L0_attn_bq', 'L0_attn_Wk', 'L0_attn_bk', 'L0_attn_Wv',
        'L0_attn_bv', 'L0_attn_Wo', 'L0_attn_bo', 'L0_attn_Wq_lsr', 'L0_attn_Wk_lsr', 'L0_xattn_qkv_w',
        'L0_xattn_proj_w', 'L0_xattn_proj_b', 'L0_ffn_W_r', 'L0_ffn_W_k', 'L0_ffn_W_v', 'L0_ffn_mu_r', 'L0_ffn_mu_k']


def kernel(**inputs):
    import numpy as np
    import concourse.bacc as bacc
    from concourse import mybir as _mybir
    from concourse.bass_utils import run_bass_kernel_spmd

    nc = bacc.Bacc("TRN2", target_bir_lowering=False, num_devices=1)
    arrays, args = {}, []
    for name in _INS:
        a = np.ascontiguousarray(inputs[name])
        arrays[f"in_{name}"] = a
        args.append(nc.dram_tensor(f"in_{name}", a.shape, _mybir.dt.from_np(a.dtype), kind="ExternalInput").ap())
    shape = np.shape(inputs['x'])
    args.append(nc.dram_tensor("out_x", shape, _mybir.dt.float32, kind="ExternalOutput").ap())
    decoder_layer(nc, *args)
    r = run_bass_kernel_spmd(nc, [arrays], core_ids=[0])
    return r.results[0]["out_x"]
```

```python
from contextlib import ExitStack

import concourse.bass as bass
from concourse import mybir

F32 = mybir.dt.float32
F32R = mybir.dt.float32r
BF16 = mybir.dt.bfloat16
F16 = mybir.dt.float16
I32 = mybir.dt.int32
ALU = mybir.AluOpType
ACT = mybir.ActivationFunctionType
AX_X = mybir.AxisListType.X

P = 128
RING = 3
HEADS, DH, RANK = 16, 16, 32
EPS = 1e-5
MASKED = -1e30
LN2_12 = 8.317766166719343
XATTN_HEADS = 8

IN, SCORES, PROBS, CROSS, FFN = range(5)
LAST_SKEW = FFN
ONES_ROW = 48
STACK_ROWS = ONES_ROW + 2


class Batch:

    def __init__(self, turn, at, skew):
        self.n = 3 * turn + (at - skew)
        self.slot = (at - skew) % RING
        self.turn = turn + (at - skew) // RING
        self.static = isinstance(turn, int)

    def dma_count(self, dmas, back=0):
        return (self.turn + (1 - back)) * (16 * dmas)


def decoder_layer(nc, x, ctx_in, mask_in, Wq, bq, Wk, bk, Wv, bv, Wo, bo, Wq_lsr, Wk_lsr,
                  qkv_w, proj_w, proj_b, W_r, W_k, W_v, mu_r, mu_k, out):
    B, T, C = x.shape
    M = ctx_in.shape[1]
    NT, KC = T // P, C // P
    XSCALE = float(C // XATTN_HEADS) ** -0.5
    assert NT == 2 and KC == 2 and M <= P and C == HEADS * DH

    es = ExitStack()
    with es:
        def sb(name, shape, dt=F32):
            return es.enter_context(nc.sbuf_tensor(name, shape, dt))

        def ps(name, shape, dt=F32):
            return es.enter_context(nc.psum_tensor(name, shape, dt))

        def sem(name):
            return es.enter_context(nc.semaphore(name))

        ident = sb("ident", [P, P])
        identb = sb("identb", [P, P], BF16)
        mask_s = sb("mask_s", [P, 4, P], BF16)
        mask_t = sb("mask_t", [P, 4, P], BF16)
        ones_row = sb("ones_row", [1, P])
        neg_half = sb("neg_half", [P, NT])
        eps = sb("eps", [P, NT])
        minus_one = sb("minus_one", [P, NT])
        pause = sb("pause", [P, 1])
        raw_names = ["Wk", "Wv", "Wq", "Wo", "Wxv", "Wp", "Wr", "Wkf", "Wvf", "Wxq", "Wxk"]
        raw_dram = {"Wq": Wq, "Wk": Wk, "Wv": Wv, "Wo": Wo, "Wxq": qkv_w[0:C, :], "Wxk": qkv_w[C:2 * C, :],
                    "Wxv": qkv_w[2 * C:3 * C, :], "Wp": proj_w, "Wr": W_r, "Wkf": W_k, "Wvf": W_v}
        turned_names = ["Wk", "Wv", "Wo", "Wxv", "Wp", "Wr", "Wkf", "Wvf"]
        SPLIT = ("Wq", "Wk", "Wv", "Wo")
        wT = {n: sb("T_" + n, [P, KC, C]) for n in turned_names if n not in SPLIT}
        w_hi = {n: sb("hi_" + n, [P, KC, C], F32R) for n in SPLIT}
        w_lo = {n: sb("lo_" + n, [P, KC, C], F32R) for n in SPLIT}
        wx_fold = sb("wx_fold", [P, KC, C])
        cols = sb("cols", [P, 5, KC])
        BQ, BK, BV, MUR, MUK = range(5)
        bq_fold = sb("bq_fold", [P, KC])
        c1 = sb("c1", [P, C])
        pb_rep = sb("pb_rep", [P, C])
        mask_i = sb("mask_i", [M, 1], I32)
        keep = sb("keep", [M, 1])

        x_in = [sb(f"x_in{r}", [P, NT, C]) for r in range(RING)]
        xT = [[sb(f"xT_{part}{r}", [P, KC, T], F32R) for part in ("hi", "lo")] for r in range(RING)]
        parts = [sb(f"parts{s}", [P, KC, 2, T], F32R) for s in range(2)]
        stack = [[sb(f"stack{s}_{r}", [P, HEADS // 2, T], F32R) for r in range(RING)] for s in range(2)]
        row_max = sb("row_max", [P, NT, 2, HEADS // 2])
        shift = sb("shift", [HEADS, T])
        shift_parts = sb("shift_parts", [HEADS, 2, T], F32R)
        v_parts = [sb(f"v_parts{r}", [P, NT, HEADS, 3, DH + 1], BF16) for r in range(RING)]
        v_rest = sb("v_rest", [P, NT, C])
        p32 = [sb(f"p32_{i}", [P, 1024]) for i in range(3)]
        p_hi = [sb(f"p_hi{i}", [P, 1024], F16) for i in range(6)]
        p_lo = [sb(f"p_lo{i}", [P, 1024], F16) for i in range(6)]
        lsrT = p32[0][0:RANK, 0:512].rearrange("r (s a p) -> r s a p", s=2, a=KC)
        lsr_prod = p32[0][:, 512:768].rearrange("p (a b) -> p a b", a=KC)
        bv_rep = p32[0][:, 768:1024].rearrange("p (a b) -> p a b", a=KC)
        lsr = p32[1][:, 0:128].rearrange("p (s a r) -> p s a r", s=2, a=KC)
        block_diag = p32[1][:, 128:256]
        rows = p32[1][0:1, 256:768].rearrange("o (i c) -> o i c", i=2)
        raw = {n: t[:].bitcast(F32).rearrange("p (a c) -> p a c", a=KC) for n, t in zip(raw_names, p_hi + p_lo)}
        o_sum = sb("o_sum", [P, NT, HEADS // 2, DH + 1])
        o_rec = sb("o_rec", [P, NT, HEADS // 2])
        y = sb("y", [P, NT, HEADS, DH])
        yT = [sb("yT_" + part, [P, KC, T], F32R) for part in ("hi", "lo")]
        ctx_sb = sb("ctx_sb", [M, C])
        ctxT = sb("ctxT", [P, KC, M])
        kxT = [sb(f"kxT{r}", [P, KC, M]) for r in range(RING)]
        vx = [sb(f"vx{r}", [M, C]) for r in range(RING)]
        x_res = sb("x_res", [P, NT, C])
        sum1 = sb("sum1", [P, NT, C])
        sum2 = sb("sum2", [P, NT, C])
        sum3 = sb("sum3", [P, NT, C])
        bn = [sb(f"bn{i}", [P, NT, 6]) for i in range(3)]
        mv = [sb(f"mv{i}", [P, NT, 2]) for i in range(3)]
        var = [sb(f"var{i}", [P, NT]) for i in range(3)]
        rstd = [sb(f"rstd{i}", [P, NT]) for i in range(3)]
        neg_mean = [sb(f"neg_mean{i}", [P, NT]) for i in range(3)]
        offset = [sb(f"offset{i}", [P, NT]) for i in range(3)]
        x1 = sum1
        x1p = sb("x1p", [P, NT, C])
        x1T = sb("x1T", [P, KC, T])
        s2_max = sb("s2_max", [P, NT])
        s2_neg = sb("s2_neg", [P, NT])
        s2_sum = sb("s2_sum", [P, NT])
        s2_rec = sb("s2_rec", [P, NT])
        a_exp = sb("a_exp", [P, NT, M])
        a_nrm = sb("a_nrm", [P, NT, M])
        g_sb = sb("g_sb", [M, C])
        x2 = sb("x2", [P, NT, C])
        x2T = sb("x2T", [P, KC, 1 + T])
        dx = sb("dx", [P, KC, T])
        xr = sb("xr", [P, KC, T])
        xk = sb("xk", [P, KC, T])
        k_relu = sb("k_relu", [P, KC, T])
        k_act = k_relu
        r_tanh = sb("r_tanh", [P, NT, C])
        gated = r_tanh
        x3 = sum3

        parts_dram = [[nc.dram_tensor(f"parts_dram{s}_{r}", [KC * P, 2, T], F32, kind="Internal").ap()
                       for r in range(RING)] for s in range(2)]

        ps_s = ps("ps_s", [P, 1024])
        ps_t = ps("ps_t", [P, 1024])
        ps_o = ps("ps_o", [P, NT, 512])
        ps_m = [ps(f"ps_m{i}", [P, 512]) for i in range(2)]

        setup_banks = [t for w in (ps_s, ps_t) for t in (w[:, 0:512], w[:, 512:1024])] + \
            [ps_o[:, 0, :], ps_o[:, 1, :], ps_m[0][:], ps_m[1][:]]

        def sems(*names):
            return {n: sem(n) for n in names}

        filled = sems(*["f_" + n for n in ("xT", "q", "k", "v", "mT", "yT", "z1", "x1T", "s2", "g", "z2", "ctxT",
                                           "kx", "vx", "x2T", "k3", "r3", "v3")])
        s_filled = [sem(f"s_filled{c}") for c in range(6)]
        t_filled = [sem(f"t_filled{c}") for c in range(6)]
        o_filled = [sem(f"o_filled{c}") for c in range(2)]
        exp_done = [sem(f"exp_done{c}") for c in range(6)]
        a_ = sems("xT_hi", "q_hi", "k_hi", "v_hi", "v_mid", "yT_hi", "x1T_ready", "a_exp_done", "g_ready",
                  "vx_ready", "x2T_ready", "k_relu_done", "r_tanh_done", "k_act_ready", "ctxT_ready", "kxT_ready",
                  "x1_ready", "x2_ready", "x3_ready")
        max_done = [sem(f"max_done{c}") for c in range(6)]
        p_hi_done = [sem(f"p_hi_done{c}") for c in range(6)]
        o_summed = [sem(f"o_summed{c}") for c in range(2)]
        o_inverse = [sem(f"o_inverse{c}") for c in range(2)]
        y_ready = [sem(f"y_ready{c}") for c in range(2)]
        v_ = sems("xT_lo", "yT_lo", "q_lo", "k_lo", "v_rest_done", "shift_done", "shift_hi", "shift_lo",
                  "s2_max_done", "s2_neg_done", "s2_rec_done", "a_ready", "sum1_done", "sum2_done", "sum3_done",
                  "gated_done", "xr_ready", "xk_ready")
        bn_done = [sem(f"bn_done{i}") for i in range(3)]
        mv_done = [sem(f"mv_done{i}") for i in range(3)]
        p_lo_done = [sem(f"p_lo_done{c}") for c in range(6)]
        g_ = sems("x_c_ready", "x1p_ready", "v_lo", "dx_done")
        var_done = [sem(f"var_done{i}") for i in range(3)]
        rstd_done = [sem(f"rstd_done{i}") for i in range(3)]
        neg_mean_done = [sem(f"neg_mean_done{i}") for i in range(3)]
        offset_done = [sem(f"offset_done{i}") for i in range(3)]
        x_loaded = [sem(f"x_loaded{r}") for r in range(RING)]
        parts_saved = [[sem(f"parts_saved{s}_{r}") for r in range(RING)] for s in range(2)]
        stack_loaded = [sem(f"stack_loaded{r}") for r in range(RING)]
        shift_loaded = [sem(f"shift_loaded{r}") for r in range(RING)]
        ctx_loaded = sem("ctx_loaded")
        x_res_loaded = sem("x_res_loaded")
        out_saved = sem("out_saved")
        loaded_first, loaded_rest = sem("loaded_first"), sem("loaded_rest")
        raw_loaded = {n: (loaded_first, 16 * 4) if i < 4 else (loaded_rest, 16 * (len(raw_names) - 4))
                      for i, n in enumerate(raw_names)}
        lsr_loaded = sem("lsr_loaded")
        small_loaded = sem("small_loaded")
        consts_ready = sem("consts_ready")
        consts_step = sem("consts_step")
        dve_consts = sem("dve_consts")
        ident_ready = sem("ident_ready")
        block_diag_ready = sem("block_diag_ready")
        v_zeroed = sem("v_zeroed")
        w_split = sem("w_split")
        setup_filled = sem("setup_filled")
        setup_taken = sem("setup_taken")

        def wait(eng, s, count):
            if not isinstance(count, int) or count > 0:
                eng.wait_ge(s, count)

        BANK_USERS = [
            [("xT", IN, v_["xT_lo"]), ("z1", CROSS, v_["sum1_done"]), ("x2T", FFN, a_["x2T_ready"]),
             ("x1T", CROSS, a_["x1T_ready"]), ("s2", CROSS, a_["a_exp_done"]), ("r3", FFN, a_["r_tanh_done"]),
             ("mT", SCORES, v_["shift_done"]), ("v3", FFN, v_["gated_done"]), ("kx", PROBS, a_["kxT_ready"])],
            [("yT", CROSS, v_["yT_lo"]), ("q", IN, v_["q_lo"]), ("k", IN, v_["k_lo"]),
             ("v", SCORES, v_["v_rest_done"]), ("k3", FFN, a_["k_relu_done"]), ("g", CROSS, a_["g_ready"]),
             ("ctxT", PROBS, a_["ctxT_ready"]), ("z2", CROSS, v_["sum2_done"]), ("vx", PROBS, a_["vx_ready"])],
        ]
        WHERE = {u[0]: (bank, i) for bank in range(2) for i, u in enumerate(BANK_USERS[bank])}

        def bank_of(what):
            return ps_m[WHERE[what][0]]

        def bank_free(pe, what, turn, at):
            bank, i = WHERE[what]
            users = BANK_USERS[bank]
            for back in range(1, 3 * len(users)):
                j = (i - back) % len(users)
                _, skew, read = users[j]
                at_j = at + (i - back - j) // len(users)
                b = Batch(turn, at_j, skew)
                if not b.static or 0 <= b.n < B:
                    pe.wait_ge(read, b.n + 1)
                    break
            else:
                pass
            return ps_m[bank]

        NARROW, WIDE = (0, 1), (2, 3, 4, 5)
        S_ORDER = [0, 2, 3, 1, 4, 5]
        T_ORDER = [0, 2, 3, 1, 4, 5]

        def chunk_heads(c):
            return range(8 * c, 8 * c + 8) if c in NARROW else range(4 * (c - 2), 4 * (c - 2) + 4)

        def column(c, h):
            width = P if c in NARROW else T
            return 512 * (h % 2) + width * ((h - chunk_heads(c)[0]) // 2)

        def before(order, c, b):
            i = order.index(c)
            return (order[i - 1], b.n + 1) if i else (order[-1], b.n)

        block = es.enter_context(nc.Block())

        def flat(t):
            return t[:].rearrange("p a b -> p (a b)")

        def live(turn, at, skew):
            b = Batch(turn, at, skew)
            return not b.static or 0 <= b.n < B

        def run_steps(eng, step, ahead=0, late=0):
            first = LAST_SKEW + 1 + late
            loops = (B - first) // RING
            for t in range(first):
                step(t // RING, t % RING)
            q0, r0 = first // RING, first % RING
            with eng.Fori(q0, q0 + loops) as q:
                for u in range(RING):
                    step(q, r0 + u)
            for t in range(first + loops * RING, B + LAST_SKEW + ahead):
                step(t // RING, t % RING)

        @block.sync
        def _(sp):
            sp.dma_start(lsr[:, 0], Wq_lsr.rearrange("(a h) d r -> (h d) a r", a=KC)).then_inc(lsr_loaded, 16)
            sp.dma_start(lsr[:, 1], Wk_lsr.rearrange("(a h) d r -> (h d) a r", a=KC)).then_inc(lsr_loaded, 16)
            for n in raw_names:
                sp.dma_start(raw[n], raw_dram[n].rearrange("(a p) c -> p a c", p=P)).then_inc(raw_loaded[n][0], 16)
            for i, v in enumerate((bq, bk, bv, mu_r, mu_k)):
                with nc.allow_non_contiguous_dma(reason="256 values to a column each"):
                    sp.dma_start(cols[:, i, :], v.rearrange("(a p) -> p a", p=P)).then_inc(small_loaded, 16)
            for i, v in enumerate((bo, proj_b)):
                sp.dma_start(rows[:, i, :], v.rearrange("(o c) -> o c", o=1)).then_inc(small_loaded, 16)
            sp.dma_start(mask_i[:], mask_in.rearrange("(m o) -> m o", o=1)).then_inc(small_loaded, 16)
            sp.wait_ge(consts_ready, 1)

            def tokens(ap, n):
                return ap[n, :, :] if isinstance(n, int) else ap[bass.ds(n, 1), :, :].rearrange("o t c -> (o t) c")

            def load_x(b):
                wait(sp, filled["f_xT"], b.n - 2)
                sp.dma_start(x_in[b.slot][:], tokens(x, b.n).rearrange("(j p) c -> p j c", p=P)) \
                    .then_inc(x_loaded[b.slot], 16)

            def step(turn, at):
                if live(turn, at, IN):
                    load_x(Batch(turn, at, IN))
                at = at - 1
                b = Batch(turn, at, IN)
                if live(turn, at, PROBS):
                    c = Batch(turn, at, PROBS)
                    wait(sp, v_["sum1_done"], c.n)
                    sp.dma_start(x_res[:], tokens(x, c.n).rearrange("(j p) c -> p j c", p=P)).then_inc(x_res_loaded, 16)
                if live(turn, at, IN):
                    for s, ready in enumerate(("q_lo", "k_lo")):
                        sp.wait_ge(v_[ready], b.n + 1)
                        sp.dma_start(parts_dram[s][b.slot].rearrange("(a p) w t -> p a w t", p=P), parts[s][:].bitcast(F32)) \
                            .then_inc(parts_saved[s][b.slot], 16)
                    wait(sp, t_filled[T_ORDER[-1]], b.n - 2)
                    for s, which in enumerate(((0, 0, 1), (0, 1, 0))):
                        sp.wait_ge(parts_saved[s][b.slot], b.dma_count(1))
                        for g in range(2):
                            for row, part in enumerate(which):
                                src = parts_dram[s][b.slot].rearrange("(j g d) w t -> g w d j t", g=2, d=DH)[g, part]
                                r0 = 64 * g + DH * row
                                sp.dma_start(stack[s][b.slot][r0:r0 + DH].bitcast(F32), src) \
                                    .then_inc(stack_loaded[b.slot], 16)
                if live(turn, at, SCORES):
                    c = Batch(turn, at, SCORES)
                    wait(sp, filled["f_ctxT"], c.n)
                    sp.dma_start(ctx_sb[:], tokens(ctx_in, c.n)).then_inc(ctx_loaded, 16)
                if live(turn, at, SCORES):
                    c = Batch(turn, at, SCORES)
                    sp.wait_ge(v_["shift_lo"], c.n + 1)
                    for g in range(2):
                        for part in range(2):
                            r0 = 64 * g + ONES_ROW + part
                            sp.dma_start(stack[0][c.slot][r0:r0 + 1].bitcast(F32),
                                         shift_parts[8 * g:8 * g + 8, part, :].bitcast(F32)).then_inc(shift_loaded[c.slot], 16)
                if live(turn, at, FFN):
                    c = Batch(turn, at, FFN)
                    sp.wait_ge(a_["x3_ready"], c.n + 1)
                    sp.dma_start(tokens(out, c.n).rearrange("(j p) c -> p j c", p=P), x3[:]).then_inc(out_saved, 16)

            run_steps(sp, step, ahead=1)
            sp.wait_ge(out_saved, 16 * B)

        @block.tensor
        def _(pe):
            bank_no = [0]

            def setup_bank():
                n = bank_no[0]
                bank_no[0] += 1
                if n >= len(setup_banks):
                    pe.wait_ge(setup_taken, n + 1 - len(setup_banks))
                return setup_banks[n % len(setup_banks)]

            pe.wait_ge(ident_ready, 1)
            pe.wait_ge(lsr_loaded, 32)
            bank = setup_bank()
            for s in range(2):
                for a in range(KC):
                    i = s * KC + a
                    last = nc.tensor.transpose(bank[0:RANK, i * P:(i + 1) * P], lsr[:, s, a, :], ident[:])
            last.then_inc(setup_filled, 1)

            def turn_weight(n):
                bank = setup_bank()
                pe.wait_ge(*raw_loaded[n])
                for k in range(KC):
                    for a in range(KC):
                        last = nc.tensor.transpose(bank[:, k * C + a * P:k * C + (a + 1) * P],
                                                   raw[n][:, a, k * P:(k + 1) * P], ident[:])
                last.then_inc(setup_filled, 1)

            turn_weight("Wk")
            bank = setup_bank()
            pe.wait_ge(setup_taken, 1)
            for a in range(KC):
                last = nc.tensor.matmul(bank[:, a * P:(a + 1) * P], lsrT[:, 0, a, :], lsrT[:, 1, a, :],
                                        start=True, stop=True)
            last.then_inc(setup_filled, 1)
            turn_weight("Wv")
            pe.wait_ge(*raw_loaded["Wq"])
            pe.wait_ge(small_loaded, 16 * 8)
            bank = setup_bank()
            pe.wait_ge(setup_taken, 3)
            for k in range(KC):
                for a in range(KC):
                    last = nc.tensor.matmul(bank[:, k * C + a * P:k * C + (a + 1) * P],
                                            raw["Wq"][:, a, k * P:(k + 1) * P], lsr_prod[:, a, :], start=True, stop=True)
            last.then_inc(setup_filled, 1)
            bank = setup_bank()
            for a in range(KC):
                last = nc.tensor.matmul(bank[:, a:a + 1], lsr_prod[:, a, :], cols[:, BQ, a:a + 1], start=True, stop=True)
            last.then_inc(setup_filled, 1)
            for n in turned_names[2:]:
                turn_weight(n)
            for n in ("Wxq", "Wxk"):
                pe.wait_ge(*raw_loaded[n])
            bank = setup_bank()
            for k in range(KC):
                for a in range(KC):
                    last = nc.tensor.matmul(bank[:, k * C:(k + 1) * C], raw["Wxk"][:, a, k * P:(k + 1) * P],
                                            raw["Wxq"][:, a, :], start=(a == 0), stop=(a == KC - 1))
            last.then_inc(setup_filled, 1)
            bank = setup_bank()
            pe.wait_ge(dve_consts, 1)
            pe.wait_ge(consts_ready, 1)
            pe.wait_ge(setup_taken, 7)
            for a in range(KC):
                for e, part in enumerate((w_hi["Wo"], w_lo["Wo"])):
                    nc.tensor.matmul(bank[:, 0:C], bv_rep[:, a, :], part[:, a, :].bitcast(F32),
                                     start=(a == 0 and e == 0), stop=False)
            nc.tensor.matmul(bank[:, 0:C], ones_row[:], rows[:, 0, :], start=False, stop=True).then_inc(setup_filled, 1)
            bank = setup_bank()
            nc.tensor.matmul(bank[:, 0:C], ones_row[:], rows[:, 1, :], start=True, stop=True).then_inc(setup_filled, 1)
            assert bank_no[0] == SETUP_TOTAL
            pe.wait_ge(setup_taken, SETUP_TOTAL)

            def turn_tiles(bank, src):
                for k in range(KC):
                    for j in range(NT):
                        last = nc.tensor.transpose(bank[:, k * T + j * P:k * T + (j + 1) * P],
                                                   src[:, j, k * P:(k + 1) * P], ident[:])
                return last

            def rows_out(bank, w, src):
                n = src.shape[-1]
                for a in range(KC):
                    for k in range(KC):
                        last = nc.tensor.matmul(bank[:, a * n:(a + 1) * n], w[:, k, a * P:(a + 1) * P], src[:, k, :],
                                                start=(k == 0), stop=(k == KC - 1))
                return last

            def tokens_out(bank, src, w, tiles=NT, rows=P):
                for j in range(tiles):
                    for k in range(KC):
                        last = nc.tensor.matmul(bank[0:rows, j * C:(j + 1) * C], src[:, k, j * P:j * P + rows], w[:, k, :],
                                                start=(k == 0), stop=(k == KC - 1))
                return last

            def split_terms(w, src):
                return [(w_hi[w], src[0]), (w_hi[w], src[1]), (w_lo[w], src[0])]

            def rows_out_split(bank, w, src):
                for a in range(KC):
                    terms = [(ww[:, k, a * P:(a + 1) * P], ss[:, k, :]) for k in range(KC) for ww, ss in split_terms(w, src)]
                    for e, (ww, ss) in enumerate(terms):
                        last = nc.tensor.matmul(bank[:, a * T:(a + 1) * T], ww, ss, start=(e == 0),
                                                stop=(e == len(terms) - 1))
                return last

            def tokens_out_split(bank, src, w):
                for j in range(NT):
                    terms = [(ss[:, k, j * P:(j + 1) * P], ww[:, k, :]) for k in range(KC) for ww, ss in split_terms(w, src)]
                    for e, (ss, ww) in enumerate(terms):
                        last = nc.tensor.matmul(bank[:, j * C:(j + 1) * C], ss, ww, start=(e == 0),
                                                stop=(e == len(terms) - 1))
                return last

            def scores(b, c, target, free, free_count, done, left, right, mask):
                wait(pe, free, free_count)
                heads = chunk_heads(c)
                rows_at = 0 if (c in NARROW) == (left is stack[0]) else P
                width, col = (P, rows_at) if c in NARROW else (T, 0)
                for h in heads:
                    r0 = 64 * (h % 2)
                    at_h = column(c, h)
                    o = target[:, at_h:at_h + width]
                    first_in_bank = h - heads[0] < 2
                    rows_n = STACK_ROWS if left is stack[1] else ONES_ROW
                    nc.tensor.matmul(o, left[b.slot][r0:r0 + rows_n, h // 2, rows_at:rows_at + P],
                                     right[b.slot][r0:r0 + rows_n, h // 2, col:col + width],
                                     start=first_in_bank, stop=False, skip_group_check=True)
                for half in range(2):
                    o = target[:, half * 512:(half + 1) * 512]
                    if c in NARROW:
                        last = nc.tensor.matmul(o, identb[:], mask[:].rearrange("p a b -> p (a b)"),
                                                start=False, stop=True, skip_group_check=True)
                    else:
                        o = o.rearrange("p (n w) -> p n w", n=2)
                        o = o[:, :, P:2 * P] if left is stack[0] else o[:, :, 0:P]
                        last = nc.tensor.matmul(o, identb[:], mask[:, 0:2, :], start=False, stop=True,
                                                skip_group_check=True)
                last.then_inc(done, 1)

            def step(turn, at):
                A, Sb, Pb, X, F = (Batch(turn, at, s) for s in range(5))
                on = [live(turn, at, s) for s in range(5)]

                def S(c):
                    if on[SCORES]:
                        if c == S_ORDER[0]:
                            pe.wait_ge(stack_loaded[Sb.slot], Sb.dma_count(12))
                        prev, count = before(S_ORDER, c, Sb)
                        scores(Sb, c, ps_s, max_done[prev], count, s_filled[c], stack[0], stack[1], mask_s)

                def Tr(c):
                    if on[PROBS]:
                        if c == T_ORDER[0]:
                            pe.wait_ge(shift_loaded[Pb.slot], Pb.dma_count(4))
                        prev, count = before(T_ORDER, c, Pb)
                        scores(Pb, c, ps_t, exp_done[prev], count, t_filled[c], stack[1], stack[0], mask_t)

                def PV(half):
                    if not on[PROBS]:
                        return
                    b = Pb
                    wait(pe, o_summed[1 - half], 2 * (b.n + half))
                    if half == 0:
                        pe.wait_ge(g_["v_lo"], b.n + 1)
                    for c in (half, 2 + 2 * half, 3 + 2 * half):
                        pe.wait_ge(p_lo_done[c], b.n + 1)
                    for h8 in range(8):
                        h = 8 * half + h8
                        w = 2 + h // 4
                        cw, cn = column(w, h), column(half, h)
                        v = [v_parts[b.slot][:, j, h].rearrange("p a d -> p (a d)") for j in range(2)]
                        n = v[0].shape[-1]
                        for i in range(NT):
                            o = ps_o[:, i, h8 * n:(h8 + 1) * n]
                            terms = [(p[w][:, cw + i * P:cw + (i + 1) * P], v[0]) for p in (p_hi, p_lo)]
                            if i == 1:
                                terms += [(p[half][:, cn:cn + P], v[1]) for p in (p_hi, p_lo)]
                            for e, (p, vv) in enumerate(terms):
                                last = nc.tensor.matmul(o, p, vv, start=(e == 0), stop=(e == len(terms) - 1),
                                                        skip_group_check=True)
                    last.then_inc(o_filled[half], 1)

                if on[IN]:
                    bank = bank_free(pe, "xT", turn, at)
                    pe.wait_ge(x_loaded[A.slot], A.dma_count(1))
                    turn_tiles(bank, x_in[A.slot]).then_inc(filled["f_xT"], 1)
                S(0)
                if on[CROSS]:
                    bank = bank_free(pe, "yT", turn, at)
                    pe.wait_ge(y_ready[1], X.n + 1)
                    turn_tiles(bank, y[:].rearrange("p j h d -> p j (h d)")).then_inc(filled["f_yT"], 1)
                Tr(0)
                S(2)
                if on[CROSS]:
                    bank = bank_free(pe, "z1", turn, at)
                    pe.wait_ge(v_["yT_lo"], X.n + 1)
                    tokens_out_split(bank, yT, "Wo").then_inc(filled["f_z1"], 1)
                Tr(2)
                if on[IN]:
                    bank = bank_free(pe, "q", turn, at)
                    pe.wait_ge(v_["xT_lo"], A.n + 1)
                    rows_out_split(bank, "Wq", xT[A.slot]).then_inc(filled["f_q"], 1)
                if on[FFN]:
                    bank = bank_free(pe, "x2T", turn, at)
                    pe.wait_ge(a_["x2_ready"], F.n + 1)
                    turn_tiles(bank, x2).then_inc(filled["f_x2T"], 1)
                S(3)
                Tr(3)
                if on[IN]:
                    bank = bank_free(pe, "k", turn, at)
                    rows_out_split(bank, "Wk", xT[A.slot]).then_inc(filled["f_k"], 1)
                S(1)
                Tr(1)
                if on[CROSS]:
                    bank = bank_free(pe, "x1T", turn, at)
                    pe.wait_ge(a_["x1_ready"], X.n + 1)
                    turn_tiles(bank, x1).then_inc(filled["f_x1T"], 1)
                if on[SCORES]:
                    bank = bank_free(pe, "v", turn, at)
                    pe.wait_ge(v_["xT_lo"], Sb.n + 1)
                    tokens_out_split(bank, xT[Sb.slot], "Wv").then_inc(filled["f_v"], 1)
                S(4)
                Tr(4)
                if on[CROSS]:
                    bank = bank_free(pe, "s2", turn, at)
                    pe.wait_ge(a_["x1T_ready"], X.n + 1)
                    pe.wait_ge(a_["kxT_ready"], X.n + 1)
                    for j in range(NT):
                        for k in range(KC):
                            last = nc.tensor.matmul(bank[:, j * M:(j + 1) * M], x1T[:, k, j * P:(j + 1) * P],
                                                    kxT[X.slot][:, k, :], start=(k == 0), stop=(k == KC - 1))
                    last.then_inc(filled["f_s2"], 1)
                if on[FFN]:
                    bank = bank_free(pe, "k3", turn, at)
                    pe.wait_ge(v_["xk_ready"], F.n + 1)
                    rows_out(bank, wT["Wkf"], xk).then_inc(filled["f_k3"], 1)
                S(5)
                Tr(5)
                if on[FFN]:
                    bank = bank_free(pe, "r3", turn, at)
                    pe.wait_ge(v_["xr_ready"], F.n + 1)
                    tokens_out(bank, xr, wT["Wr"]).then_inc(filled["f_r3"], 1)
                if on[CROSS]:
                    bank = bank_free(pe, "g", turn, at)
                    pe.wait_ge(v_["a_ready"], X.n + 1)
                    for k in range(KC):
                        last = nc.tensor.matmul(bank[0:M, 0:C], a_nrm[:, k, :], wT["Wp"][:, k, :],
                                                start=(k == 0), stop=(k == KC - 1))
                    last.then_inc(filled["f_g"], 1)
                if on[SCORES]:
                    bank = bank_free(pe, "mT", turn, at)
                    pe.wait_ge(max_done[5], Sb.n + 1)
                    for i in range(NT):
                        last = nc.tensor.transpose(bank[0:HEADS, i * P:(i + 1) * P],
                                                   row_max[:, i].rearrange("p g j -> p (g j)"), ident[:])
                    last.then_inc(filled["f_mT"], 1)
                PV(0)
                if on[PROBS]:
                    bank = bank_free(pe, "ctxT", turn, at)
                    pe.wait_ge(ctx_loaded, (Pb.n + 1) * 16)
                    for k in range(KC):
                        last = nc.tensor.transpose(bank[:, k * M:(k + 1) * M], ctx_sb[:, k * P:(k + 1) * P],
                                                   ident[0:M, 0:M])
                    last.then_inc(filled["f_ctxT"], 1)
                if on[FFN]:
                    bank = bank_free(pe, "v3", turn, at)
                    pe.wait_ge(a_["k_act_ready"], F.n + 1)
                    tokens_out(bank, k_act, wT["Wvf"]).then_inc(filled["f_v3"], 1)
                if on[CROSS]:
                    bank = bank_free(pe, "z2", turn, at)
                    pe.wait_ge(a_["g_ready"], X.n + 1)
                    pe.wait_ge(a_["vx_ready"], X.n + 1)
                    for j in range(NT):
                        last = nc.tensor.matmul(bank[:, j * C:(j + 1) * C], vx[X.slot][:, j * P:(j + 1) * P], g_sb[:],
                                                start=True, stop=True)
                    last.then_inc(filled["f_z2"], 1)
                if on[PROBS]:
                    bank = bank_free(pe, "kx", turn, at)
                    pe.wait_ge(a_["ctxT_ready"], Pb.n + 1)
                    rows_out(bank, wx_fold, ctxT).then_inc(filled["f_kx"], 1)
                PV(1)
                if on[PROBS]:
                    bank = bank_free(pe, "vx", turn, at)
                    tokens_out(bank, ctxT, wT["Wxv"], tiles=1, rows=M).then_inc(filled["f_vx"], 1)

            run_steps(pe, step)

        @block.scalar
        def _(act):
            def step(turn, at):
                A, Sb, Pb, X, F = (Batch(turn, at, s) for s in range(5))
                on = [live(turn, at, s) for s in range(5)]

                def exp(c):
                    if not on[PROBS]:
                        return
                    i = T_ORDER.index(c)
                    act.wait_ge(t_filled[c], Pb.n + 1)
                    prev, count = (T_ORDER[i - 3], Pb.n + 1) if i >= 3 else (T_ORDER[i + 3], Pb.n)
                    wait(act, p_lo_done[prev], count)
                    nc.scalar.activation(p32[i % 3][:], ps_t[:], ACT.Exp).then_inc(exp_done[c], 1)

                def split_hi(b, s, name, bias, what):
                    act.wait_ge(filled["f_" + what], b.n + 1)
                    prev = Batch(turn, at - 1, IN)
                    if not prev.static or prev.n >= 0:
                        act.wait_ge(parts_saved[s][prev.slot], prev.dma_count(1))
                    bank = ps_m[WHERE[what][0]]
                    for a in range(KC):
                        last = nc.scalar.activation(parts[s][:, a, 0, :], bank[:, a * T:(a + 1) * T], ACT.Identity,
                                                    bias=bias[a])
                    last.then_inc(a_[name], 1)

                def normalise(i, b, dst, src, done):
                    act.wait_ge(offset_done[i], b.n + 1)
                    for j in range(NT):
                        last = nc.scalar.activation(dst[:, j, :], src[:, j, :], ACT.Identity, bias=offset[i][:, j:j + 1],
                                                    scale=rstd[i][:, j:j + 1])
                    last.then_inc(a_[done], 1)

                def copy_high(c):
                    if on[PROBS]:
                        act.wait_ge(exp_done[c], Pb.n + 1)
                        wait(act, o_filled[1], Pb.n)
                        nc.scalar.copy(p_hi[c][:], p32[T_ORDER.index(c) % 3][:]).then_inc(p_hi_done[c], 1)

                if on[IN]:
                    act.wait_ge(filled["f_xT"], A.n + 1)
                    wait(act, filled["f_v"], A.n - 2)
                    nc.scalar.copy(flat(xT[A.slot][0]), bank_of("xT")[:]).then_inc(a_["xT_hi"], 1)
                if on[CROSS]:
                    act.wait_ge(filled["f_yT"], X.n + 1)
                    wait(act, filled["f_z1"], X.n)
                    nc.scalar.copy(flat(yT[0]), bank_of("yT")[:]).then_inc(a_["yT_hi"], 1)
                X1, F1 = Batch(turn, at - 1, CROSS), Batch(turn, at - 1, FFN)
                exp(0)
                if live(turn, at - 1, CROSS):
                    wait(act, v_["sum3_done"], X1.n)
                    normalise(1, X1, x2, sum2, "x2_ready")
                if live(turn, at - 1, FFN):
                    normalise(2, F1, x3, sum3, "x3_ready")
                exp(2)
                if on[IN]:
                    split_hi(A, 0, "q_hi", [bq_fold[:, a:a + 1] for a in range(KC)], "q")
                if on[FFN]:
                    act.wait_ge(filled["f_x2T"], F.n + 1)
                    wait(act, v_["xr_ready"], F.n)
                    nc.scalar.copy(x2T[:, :, 1:1 + T], bank_of("x2T")[:].rearrange("p (a b) -> p a b", a=KC)) \
                        .then_inc(a_["x2T_ready"], 1)
                exp(3)
                if on[CROSS]:
                    wait(act, filled["f_x1T"], X.n)
                    wait(act, g_["x1p_ready"], X.n)
                    normalise(0, X, x1, sum1, "x1_ready")
                if on[IN]:
                    split_hi(A, 1, "k_hi", [cols[:, BK, a:a + 1] for a in range(KC)], "k")
                exp(1)
                if on[CROSS]:
                    act.wait_ge(filled["f_x1T"], X.n + 1)
                    wait(act, filled["f_s2"], X.n)
                    nc.scalar.copy(flat(x1T), bank_of("x1T")[:]).then_inc(a_["x1T_ready"], 1)
                if on[SCORES]:
                    act.wait_ge(filled["f_v"], Sb.n + 1)
                    wait(act, o_filled[1], Sb.n - 2)
                    for j in range(NT):
                        last = nc.scalar.copy(v_parts[Sb.slot][:, j, :, 0, 0:DH],
                                              bank_of("v")[:, j * C:(j + 1) * C].rearrange("p (h d) -> p h d", h=HEADS))
                    last.then_inc(a_["v_hi"], 1)
                exp(4)
                copy_high(4)
                if on[SCORES]:
                    act.wait_ge(v_["v_rest_done"], Sb.n + 1)
                    for j in range(NT):
                        last = nc.scalar.copy(v_parts[Sb.slot][:, j, :, 1, 0:DH],
                                              v_rest[:, j, :].rearrange("p (h d) -> p h d", h=HEADS))
                    last.then_inc(a_["v_mid"], 1)
                if on[CROSS]:
                    act.wait_ge(v_["s2_neg_done"], X.n + 1)
                    wait(act, v_["a_ready"], X.n)
                    for j in range(NT):
                        last = nc.scalar.activation(a_exp[:, j, :], bank_of("s2")[:, j * M:(j + 1) * M], ACT.Exp,
                                                    bias=s2_neg[:, j:j + 1], scale=XSCALE, accum_out=s2_sum[:, j:j + 1])
                    last.then_inc(a_["a_exp_done"], 1)
                if on[FFN]:
                    act.wait_ge(filled["f_k3"], F.n + 1)
                    wait(act, filled["f_v3"], F.n)
                    nc.scalar.activation(flat(k_relu), bank_of("k3")[:], ACT.Relu).then_inc(a_["k_relu_done"], 1)
                exp(5)
                if on[FFN]:
                    act.wait_ge(a_["k_relu_done"], F.n + 1)
                    nc.scalar.activation(flat(k_act), flat(k_relu), ACT.Square).then_inc(a_["k_act_ready"], 1)
                if on[FFN]:
                    act.wait_ge(filled["f_r3"], F.n + 1)
                    wait(act, v_["sum3_done"], F.n)
                    nc.scalar.activation(flat(r_tanh), bank_of("r3")[:], ACT.Tanh, scale=0.5) \
                        .then_inc(a_["r_tanh_done"], 1)
                copy_high(5)
                if on[CROSS]:
                    act.wait_ge(filled["f_g"], X.n + 1)
                    wait(act, filled["f_z2"], X.n)
                    nc.scalar.activation(g_sb[:], bank_of("g")[0:M, 0:C], ACT.Copy, scale=keep[:]) \
                        .then_inc(a_["g_ready"], 1)
                if on[PROBS]:
                    act.wait_ge(filled["f_ctxT"], Pb.n + 1)
                    wait(act, filled["f_vx"], Pb.n)
                    nc.scalar.copy(flat(ctxT), bank_of("ctxT")[:, 0:KC * M]).then_inc(a_["ctxT_ready"], 1)
                    act.wait_ge(filled["f_kx"], Pb.n + 1)
                    wait(act, filled["f_s2"], Pb.n - 2)
                    nc.scalar.copy(flat(kxT[Pb.slot]), bank_of("kx")[:, 0:KC * M]).then_inc(a_["kxT_ready"], 1)
                if on[PROBS]:
                    act.wait_ge(filled["f_vx"], Pb.n + 1)
                    wait(act, filled["f_z2"], Pb.n - 2)
                    nc.scalar.copy(vx[Pb.slot][:], bank_of("vx")[0:M, 0:C]).then_inc(a_["vx_ready"], 1)

            act.wait_ge(setup_taken, SETUP_TOTAL)
            run_steps(act, step, ahead=1)

        @block.vector
        def _(dve):
            taken, splits = [0], [0]

            def setup_take():
                n = taken[0]
                dve.wait_ge(setup_filled, n + 1)
                taken[0] += 1
                return setup_banks[n % len(setup_banks)]

            def split_bank(n):
                bank = setup_take()
                nc.vector.tensor_copy(flat(w_hi[n]), bank).then_inc(w_split, 1)
                splits[0] += 1
                dve.wait_ge(w_split, splits[0])
                nc.vector.tensor_tensor(flat(w_lo[n]), bank, flat(w_hi[n]).bitcast(F32), ALU.subtract) \
                    .then_inc(setup_taken, 1)

            def copy_bank(dst):
                bank = setup_take()
                nc.vector.tensor_copy(dst, bank[:, 0:dst.shape[-1]]).then_inc(setup_taken, 1)

            for r in range(RING):
                nc.vector.memset(v_parts[r][:, :, :, :, DH:DH + 1], 0.0).then_inc(v_zeroed, 1)
            dve.wait_ge(v_zeroed, RING)
            for r in range(RING):
                nc.vector.memset(v_parts[r][:, :, :, 0, DH:DH + 1], 1.0).then_inc(v_zeroed, 1)
            dve.wait_ge(ident_ready, 1)
            dve.wait_ge(small_loaded, 16 * 8)
            nc.vector.tensor_scalar(keep[:], mask_i[:], 0.0, None, ALU.not_equal)
            for a in range(KC):
                last = nc.vector.tensor_scalar(bv_rep[:, a, :], ident[:], 0.0, cols[:, BV, a:a + 1], ALU.mult, ALU.add)
            last.then_inc(dve_consts, 1)
            bank = setup_take()
            nc.vector.tensor_copy(p32[0][0:RANK, 0:512], bank[0:RANK, :]).then_inc(setup_taken, 1)
            split_bank("Wk")
            bank = setup_take()
            dve.wait_ge(block_diag_ready, 1)
            for a in range(KC):
                last = nc.vector.scalar_tensor_tensor(lsr_prod[:, a, :], bank[:, a * P:(a + 1) * P], float(RANK) ** -0.5,
                                                      block_diag, op0=ALU.mult, op1=ALU.mult)
            last.then_inc(setup_taken, 1)
            split_bank("Wv")
            split_bank("Wq")
            copy_bank(bq_fold[:])
            split_bank("Wo")
            for n in turned_names[3:]:
                copy_bank(flat(wT[n]))
            copy_bank(flat(wx_fold))
            copy_bank(c1[:])
            copy_bank(pb_rep[:])
            assert taken[0] == SETUP_TOTAL
            dve.wait_ge(setup_taken, SETUP_TOTAL)
            dve.wait_ge(consts_ready, 1)

            def step(turn, at):
                A, Sb, Pb, X, F = (Batch(turn, at, s) for s in range(5))
                on = [live(turn, at, s) for s in range(5)]

                def row_maxima(c):
                    if not on[SCORES]:
                        return
                    dve.wait_ge(s_filled[c], Sb.n + 1)
                    if c == S_ORDER[0]:
                        wait(dve, filled["f_mT"], Sb.n)
                    heads = chunk_heads(c)
                    tile = 0 if c in NARROW else 1
                    j0, nj = heads[0] // 2, len(heads) // 2
                    nc.vector.tensor_reduce(row_max[:, tile, :, j0:j0 + nj],
                                            ps_s[:].rearrange("p (g j w) -> p g j w", j=nj, g=2), AX_X, ALU.max) \
                        .then_inc(max_done[c], 1)

                def high_part(c):
                    if not on[PROBS]:
                        return
                    dve.wait_ge(exp_done[c], Pb.n + 1)
                    half = c if c in NARROW else (c - 2) // 2
                    wait(dve, o_filled[half], Pb.n)
                    nc.vector.tensor_copy(p_hi[c][:], p32[T_ORDER.index(c) % 3][:]).then_inc(p_hi_done[c], 1)

                def split_lo(b, s, hi, lo, bias, what):
                    dve.wait_ge(a_[hi], b.n + 1)
                    bank = ps_m[WHERE[what][0]]
                    for a in range(KC):
                        last = nc.vector.scalar_tensor_tensor(parts[s][:, a, 1, :], bank[:, a * T:(a + 1) * T], bias[a],
                                                              parts[s][:, a, 0, :].bitcast(F32),
                                                              op0=ALU.add, op1=ALU.subtract)
                    last.then_inc(v_[lo], 1)

                def stats(i, b, src, summed):
                    dve.wait_ge(summed, b.n + 1)
                    wait(dve, mv_done[i], b.n)
                    for j in range(NT):
                        last = nc.vector.bn_stats(bn[i][:, j, :], src[:, j, :])
                    last.then_inc(bn_done[i], 1)
                    dve.wait_ge(bn_done[i], b.n + 1)
                    wait(dve, offset_done[i], b.n)
                    nc.vector.memset(pause[:], 0.0)
                    for j in range(NT):
                        last = nc.vector.bn_aggr(mv[i][:, j, :], bn[i][:, j, :])
                    last.then_inc(mv_done[i], 1)

                def attention_out(half):
                    if not on[PROBS]:
                        return
                    b = Pb
                    dve.wait_ge(o_filled[half], b.n + 1)
                    wait(dve, y_ready[1 - half], b.n + half)
                    for i in range(NT):
                        nc.vector.tensor_reduce(o_sum[:, i],
                                                ps_o[:, i, 0:8 * 3 * (DH + 1)].rearrange("p (h a d) -> p h d a", h=8, a=3),
                                                AX_X, ALU.add).then_inc(o_summed[half], 1)
                    dve.wait_ge(o_summed[half], (b.n + 1) * 2)
                    nc.vector.reciprocal(o_rec[:], o_sum[:, :, :, DH]).then_inc(o_inverse[half], 1)
                    dve.wait_ge(o_inverse[half], b.n + 1)
                    wait(dve, filled["f_yT"], b.n)
                    for i in range(NT):
                        last = nc.vector.tensor_tensor(y[:, i, 8 * half:8 * half + 8, :], o_sum[:, i, :, 0:DH],
                                                       o_rec[:, i, :].unsqueeze(2).to_broadcast([P, 8, DH]), ALU.mult)
                    last.then_inc(y_ready[half], 1)

                def mix(dst, mu, ready, used):
                    wait(dve, filled[used], F.n)
                    for k in range(KC):
                        last = nc.vector.scalar_tensor_tensor(dst[:, k, :], dx[:, k, :], cols[:, mu, k:k + 1],
                                                              x2T[:, k, 0:T], op0=ALU.mult, op1=ALU.add)
                    last.then_inc(v_[ready], 1)

                def turned_lo(b, what, dst, used):
                    dve.wait_ge(a_[what + "_hi"], b.n + 1)
                    wait(dve, *used)
                    nc.vector.tensor_tensor(flat(dst[1]), bank_of(what)[:], flat(dst[0]).bitcast(F32), ALU.subtract) \
                        .then_inc(v_[what + "_lo"], 1)

                if on[IN]:
                    turned_lo(A, "xT", xT[A.slot], (filled["f_v"], A.n - 2))
                row_maxima(0)
                if on[CROSS]:
                    turned_lo(X, "yT", yT, (filled["f_z1"], X.n))
                if live(turn, at - 1, FFN):
                    stats(2, Batch(turn, at - 1, FFN), sum3, v_["sum3_done"])
                high_part(0)
                row_maxima(2)
                if on[CROSS]:
                    dve.wait_ge(filled["f_z1"], X.n + 1)
                    dve.wait_ge(g_["x_c_ready"], X.n + 1)
                    wait(dve, a_["x1_ready"], X.n)
                    nc.vector.tensor_tensor(flat(sum1), bank_of("z1")[:], flat(x_res), ALU.add) \
                        .then_inc(v_["sum1_done"], 1)
                    stats(0, X, sum1, v_["sum1_done"])
                high_part(2)
                if on[IN]:
                    split_lo(A, 0, "q_hi", "q_lo", [bq_fold[:, a:a + 1] for a in range(KC)], "q")
                row_maxima(3)
                high_part(3)
                if on[IN]:
                    split_lo(A, 1, "k_hi", "k_lo", [cols[:, BK, a:a + 1] for a in range(KC)], "k")
                row_maxima(1)
                if on[FFN]:
                    dve.wait_ge(g_["dx_done"], F.n + 1)
                    mix(xk, MUK, "xk_ready", "f_k3")
                if on[SCORES]:
                    dve.wait_ge(a_["v_hi"], Sb.n + 1)
                    wait(dve, g_["v_lo"], Sb.n)
                    for j in range(NT):
                        last = nc.vector.tensor_tensor(
                            v_rest[:, j, :].rearrange("p (h d) -> p h d", h=HEADS),
                            bank_of("v")[:, j * C:(j + 1) * C].rearrange("p (h d) -> p h d", h=HEADS),
                            v_parts[Sb.slot][:, j, :, 0, 0:DH], ALU.subtract)
                    last.then_inc(v_["v_rest_done"], 1)
                high_part(1)
                row_maxima(4)
                if on[FFN]:
                    mix(xr, MUR, "xr_ready", "f_r3")
                if on[CROSS]:
                    dve.wait_ge(filled["f_s2"], X.n + 1)
                    wait(dve, v_["s2_neg_done"], X.n)
                    nc.vector.tensor_reduce(s2_max[:], bank_of("s2")[:, 0:NT * M].rearrange("p (j m) -> p j m", j=NT),
                                            AX_X, ALU.max).then_inc(v_["s2_max_done"], 1)
                    dve.wait_ge(v_["s2_max_done"], X.n + 1)
                    wait(dve, a_["a_exp_done"], X.n)
                    nc.vector.tensor_scalar(s2_neg[:], s2_max[:], -XSCALE, None, ALU.mult) \
                        .then_inc(v_["s2_neg_done"], 1)
                row_maxima(5)
                if on[CROSS]:
                    dve.wait_ge(a_["a_exp_done"], X.n + 1)
                    wait(dve, v_["a_ready"], X.n)
                    nc.vector.reciprocal(s2_rec[:], s2_sum[:]).then_inc(v_["s2_rec_done"], 1)
                    dve.wait_ge(v_["s2_rec_done"], X.n + 1)
                    wait(dve, filled["f_g"], X.n)
                    for j in range(NT):
                        last = nc.vector.tensor_scalar(a_nrm[:, j, :], a_exp[:, j, :], s2_rec[:, j:j + 1], None, ALU.mult)
                    last.then_inc(v_["a_ready"], 1)
                if on[SCORES]:
                    dve.wait_ge(filled["f_mT"], Sb.n + 1)
                    wait(dve, v_["shift_lo"], Sb.n)
                    nc.vector.tensor_scalar(shift[:], bank_of("mT")[0:HEADS, 0:T], -1.0, LN2_12, ALU.mult, ALU.add) \
                        .then_inc(v_["shift_done"], 1)
                    dve.wait_ge(v_["shift_done"], Sb.n + 1)
                    prev = Batch(turn, at - 1, SCORES)
                    if not prev.static or prev.n >= 0:
                        dve.wait_ge(shift_loaded[prev.slot], prev.dma_count(4))
                    nc.vector.tensor_copy(shift_parts[:, 0, :], shift[:]).then_inc(v_["shift_hi"], 1)
                    dve.wait_ge(v_["shift_hi"], Sb.n + 1)
                    nc.vector.tensor_tensor(shift_parts[:, 1, :], shift[:], shift_parts[:, 0, :].bitcast(F32),
                                            ALU.subtract).then_inc(v_["shift_lo"], 1)
                attention_out(0)
                if on[FFN]:
                    dve.wait_ge(filled["f_v3"], F.n + 1)
                    dve.wait_ge(a_["r_tanh_done"], F.n + 1)
                    nc.vector.scalar_tensor_tensor(flat(gated), flat(r_tanh), 1.0, bank_of("v3")[:],
                                                   op0=ALU.add, op1=ALU.mult).then_inc(v_["gated_done"], 1)
                if on[CROSS]:
                    dve.wait_ge(filled["f_z2"], X.n + 1)
                    dve.wait_ge(g_["x1p_ready"], X.n + 1)
                    wait(dve, a_["x2_ready"], X.n)
                    nc.vector.tensor_tensor(flat(sum2), bank_of("z2")[:], flat(x1p), ALU.add) \
                        .then_inc(v_["sum2_done"], 1)
                if on[FFN]:
                    dve.wait_ge(v_["gated_done"], F.n + 1)
                    wait(dve, out_saved, F.n * 16)
                    nc.vector.scalar_tensor_tensor(flat(sum3), flat(gated), 0.5, flat(x2),
                                                   op0=ALU.mult, op1=ALU.add).then_inc(v_["sum3_done"], 1)
                if on[CROSS]:
                    stats(1, X, sum2, v_["sum2_done"])
                attention_out(1)

            run_steps(dve, step, ahead=1, late=1)

        @block.gpsimd
        def _(pool):
            done = [0]

            def link(ins):
                done[0] += 1
                ins.then_inc(consts_step, 1)
                pool.wait_ge(consts_step, done[0])

            g = nc.gpsimd
            link(g.memset(ident[:], 0.0))
            g.affine_select(out=ident[:], in_=ident[:], compare_op=ALU.not_equal, fill=1.0, base=0,
                            pattern=[[-1, P]], channel_multiplier=1).then_inc(ident_ready, 1)
            pool.wait_ge(ident_ready, 1)
            link(g.memset(block_diag, 1.0))
            bd = block_diag.rearrange("p (g e) -> p g e", e=DH)
            link(g.affine_select(out=bd, in_=bd, compare_op=ALU.is_ge, fill=0.0, base=0,
                                 pattern=[[-DH, P // DH], [0, DH]], channel_multiplier=1))
            g.affine_select(out=bd, in_=bd, compare_op=ALU.is_ge, fill=0.0, base=DH - 1,
                            pattern=[[DH, P // DH], [0, DH]], channel_multiplier=-1).then_inc(block_diag_ready, 1)
            for t, value in ((ones_row, 1.0), (neg_half, -0.5), (eps, EPS), (minus_one, -1.0)):
                link(g.memset(t[:], value))
            for r in range(RING):
                for h in range(2):
                    link(g.memset(stack[1][r][64 * h + 32:64 * h + 64].bitcast(F32), 1.0))
            link(g.tensor_copy(identb[:], ident[:]))
            link(g.memset(mask_s[:], 0.0))
            link(g.memset(mask_t[:], 0.0))
            link(g.affine_select(out=mask_s[:], in_=mask_s[:], compare_op=ALU.is_ge, fill=MASKED, base=0,
                                 pattern=[[0, 4], [-1, P]], channel_multiplier=1))
            link(g.affine_select(out=mask_t[:], in_=mask_t[:], compare_op=ALU.is_ge, fill=MASKED, base=0,
                                 pattern=[[0, 4], [1, P]], channel_multiplier=-1))
            g.memset(x2T[:, :, 0:1], 0.0).then_inc(consts_ready, 1)
            pool.wait_ge(setup_taken, SETUP_TOTAL)

            def low_part(c, b):
                pool.wait_ge(p_hi_done[c], b.n + 1)
                i = T_ORDER.index(c)
                g.tensor_tensor(p_lo[c][:], p32[i % 3][:], p_hi[c][:], ALU.subtract).then_inc(p_lo_done[c], 1)

            def inverse_deviation(i, b):
                pool.wait_ge(mv_done[i], b.n + 1)
                wait(pool, a_[("x1_ready", "x2_ready", "x3_ready")[i]], b.n)
                g.tensor_tensor(var[i][:], mv[i][:, :, 1], eps[:], ALU.add).then_inc(var_done[i], 1)
                g.tensor_tensor(neg_mean[i][:], mv[i][:, :, 0], minus_one[:], ALU.mult).then_inc(neg_mean_done[i], 1)
                pool.wait_ge(var_done[i], b.n + 1)
                g.tensor_tensor(rstd[i][:], var[i][:], neg_half[:], ALU.pow).then_inc(rstd_done[i], 1)
                pool.wait_ge(neg_mean_done[i], b.n + 1)
                pool.wait_ge(rstd_done[i], b.n + 1)
                g.tensor_tensor(offset[i][:], neg_mean[i][:], rstd[i][:], ALU.mult).then_inc(offset_done[i], 1)

            def step(turn, at):
                A, Sb, Pb, X, F = (Batch(turn, at, s) for s in range(5))
                on = [live(turn, at, s) for s in range(5)]
                if on[CROSS]:
                    pool.wait_ge(x_res_loaded, (X.n + 1) * 16)
                    g.tensor_tensor(x_res[:], x_res[:], c1[:].unsqueeze(1).to_broadcast([P, NT, C]), ALU.add) \
                        .then_inc(g_["x_c_ready"], 1)
                if live(turn, at - 1, FFN):
                    inverse_deviation(2, Batch(turn, at - 1, FFN))
                if on[PROBS]:
                    low_part(0, Pb)
                if on[CROSS]:
                    inverse_deviation(0, X)
                if on[PROBS]:
                    low_part(2, Pb)
                if on[FFN]:
                    pool.wait_ge(a_["x2T_ready"], F.n + 1)
                    wait(pool, v_["xr_ready"], F.n)
                    g.tensor_tensor(dx[:], x2T[:, :, 1:1 + T], x2T[:, :, 0:T], ALU.subtract) \
                        .then_inc(g_["dx_done"], 1)
                if on[PROBS]:
                    low_part(3, Pb)
                    low_part(1, Pb)
                if on[CROSS]:
                    pool.wait_ge(a_["x1_ready"], X.n + 1)
                    wait(pool, v_["sum2_done"], X.n)
                    g.tensor_tensor(x1p[:], x1[:], pb_rep[:].unsqueeze(1).to_broadcast([P, NT, C]), ALU.add) \
                        .then_inc(g_["x1p_ready"], 1)
                if on[PROBS]:
                    low_part(4, Pb)
                if on[SCORES]:
                    pool.wait_ge(a_["v_mid"], Sb.n + 1)
                    for j in range(NT):
                        last = g.tensor_tensor(v_parts[Sb.slot][:, j, :, 2, 0:DH],
                                               v_rest[:, j, :].rearrange("p (h d) -> p h d", h=HEADS),
                                               v_parts[Sb.slot][:, j, :, 1, 0:DH], ALU.subtract)
                    last.then_inc(g_["v_lo"], 1)
                if on[PROBS]:
                    low_part(5, Pb)
                if on[CROSS]:
                    inverse_deviation(1, X)

            run_steps(pool, step, ahead=1)


SETUP_TOTAL = 8 + 4 + 3


_INS = ['x', 'ctx_1024', 'mask_S2_ik0', 'L0_attn_Wq', 'L0_attn_bq', 'L0_attn_Wk', 'L0_attn_bk', 'L0_attn_Wv',
        'L0_attn_bv', 'L0_attn_Wo', 'L0_attn_bo', 'L0_attn_Wq_lsr', 'L0_attn_Wk_lsr', 'L0_xattn_qkv_w',
        'L0_xattn_proj_w', 'L0_xattn_proj_b', 'L0_ffn_W_r', 'L0_ffn_W_k', 'L0_ffn_W_v', 'L0_ffn_mu_r', 'L0_ffn_mu_k']


def kernel(**inputs):
    import numpy as np
    import concourse.bacc as bacc
    from concourse import mybir as _mybir
    from concourse.bass_utils import run_bass_kernel_spmd

    nc = bacc.Bacc("TRN2", target_bir_lowering=False, num_devices=1)
    arrays, args = {}, []
    for name in _INS:
        a = np.ascontiguousarray(inputs[name])
        arrays[f"in_{name}"] = a
        args.append(nc.dram_tensor(f"in_{name}", a.shape, _mybir.dt.from_np(a.dtype), kind="ExternalInput").ap())
    shape = np.shape(inputs['x'])
    args.append(nc.dram_tensor("out_x", shape, _mybir.dt.float32, kind="ExternalOutput").ap())
    decoder_layer(nc, *args)
    r = run_bass_kernel_spmd(nc, [arrays], core_ids=[0])
    return r.results[0]["out_x"]
```

```python
from contextlib import ExitStack

import concourse.bass as bass
from concourse import mybir

F32 = mybir.dt.float32
F32R = mybir.dt.float32r
BF16 = mybir.dt.bfloat16
F16 = mybir.dt.float16
I32 = mybir.dt.int32
ALU = mybir.AluOpType
ACT = mybir.ActivationFunctionType
AX_X = mybir.AxisListType.X

P = 128
RING = 3
HEADS, DH, RANK = 16, 16, 32
EPS = 1e-5
MASKED = -1e30
LN2_12 = 8.317766166719343
XATTN_HEADS = 8

IN, SCORES, PROBS, CROSS, FFN = range(5)
LAST_SKEW = FFN
ONES_ROW = 48
STACK_ROWS = ONES_ROW + 2


class Batch:

    def __init__(self, turn, at, skew):
        self.loop_turn, self.offset = turn, at - skew
        self.n = 3 * turn + (at - skew)
        self.slot = (at - skew) % RING
        self.turn = turn + (at - skew) // RING
        self.static = isinstance(turn, int)

    def chunks_done(self, order, c):
        n = len(order)
        return self.loop_turn * (3 * n) + (self.offset * n + order.index(c) + 1)

    def dma_count(self, dmas):
        return (self.turn + 1) * (16 * dmas)


def decoder_layer(nc, x, ctx_in, mask_in, Wq, bq, Wk, bk, Wv, bv, Wo, bo, Wq_lsr, Wk_lsr,
                  qkv_w, proj_w, proj_b, W_r, W_k, W_v, mu_r, mu_k, out):
    B, T, C = x.shape
    M = ctx_in.shape[1]
    NT, KC = T // P, C // P
    XSCALE = float(C // XATTN_HEADS) ** -0.5
    assert NT == 2 and KC == 2 and M <= P and C == HEADS * DH

    es = ExitStack()
    with es:
        def sb(name, shape, dt=F32):
            return es.enter_context(nc.sbuf_tensor(name, shape, dt))

        def ps(name, shape, dt=F32):
            return es.enter_context(nc.psum_tensor(name, shape, dt))

        def sem(name):
            return es.enter_context(nc.semaphore(name))

        ident = sb("ident", [P, P])
        identb = sb("identb", [P, P], BF16)
        mask_s = sb("mask_s", [P, 4, P], BF16)
        mask_t = sb("mask_t", [P, 4, P], BF16)
        ones_row = sb("ones_row", [1, P])
        neg_half = sb("neg_half", [P, NT])
        eps = sb("eps", [P, NT])
        minus_one = sb("minus_one", [P, NT])
        pause = sb("pause", [P, 1])
        raw_names = ["Wk", "Wq", "Wv", "Wo", "Wxv", "Wp", "Wr", "Wkf", "Wvf", "Wxq", "Wxk"]
        raw_dram = {"Wq": Wq, "Wk": Wk, "Wv": Wv, "Wo": Wo, "Wxq": qkv_w[0:C, :], "Wxk": qkv_w[C:2 * C, :],
                    "Wxv": qkv_w[2 * C:3 * C, :], "Wp": proj_w, "Wr": W_r, "Wkf": W_k, "Wvf": W_v}
        turned_names = ["Wk", "Wv", "Wo", "Wxv", "Wp", "Wr", "Wkf", "Wvf"]
        SPLIT = ("Wq", "Wk", "Wv", "Wo", "Wr", "Wkf", "Wvf")
        wT = {n: sb("T_" + n, [P, KC, C]) for n in turned_names if n not in SPLIT}
        w_hi = {n: sb("hi_" + n, [P, KC, C], F32R) for n in SPLIT}
        w_lo = {n: sb("lo_" + n, [P, KC, C], F32R) for n in SPLIT}
        wx_fold = sb("wx_fold", [P, KC, C])
        cols = sb("cols", [P, 5, KC])
        BQ, BK, BV, MUR, MUK = range(5)
        bq_fold = sb("bq_fold", [P, KC])
        c1 = sb("c1", [P, C])
        pb_rep = sb("pb_rep", [P, C])
        mask_i = sb("mask_i", [M, 1], I32)
        keep = sb("keep", [M, 1])

        x_in = sb("x_in", [P, NT, C])
        xT = [[sb(f"xT_{part}{r}", [P, KC, T], F32R) for part in ("hi", "lo")] for r in range(RING)]
        parts = [sb(f"parts{s}", [P, KC, 2, T], F32R) for s in range(2)]
        stack = [[sb(f"stack{s}_{r}", [P, HEADS // 2, T], F32R) for r in range(RING)] for s in range(2)]
        row_max = sb("row_max", [P, NT, 2, HEADS // 2])
        shift_parts = sb("shift_parts", [HEADS, 2, T], F32R)
        shift = shift_parts[:, 1, :].bitcast(F32)
        v_parts = [sb(f"v_parts{r}", [P, NT, HEADS, 3, DH + 1], BF16) for r in range(RING)]
        v_rest = sb("v_rest", [P, NT, C])
        p32 = [sb(f"p32_{i}", [P, 1024]) for i in range(3)]
        p_hi = [sb(f"p_hi{i}", [P, 1024], F16) for i in range(6)]
        p_lo = [sb(f"p_lo{i}", [P, 1024], F16) for i in range(6)]
        lsrT = p32[0][0:RANK, 0:512].rearrange("r (s a p) -> r s a p", s=2, a=KC)
        lsr_prod = p32[0][:, 512:768].rearrange("p (a b) -> p a b", a=KC)
        bv_rep = p32[0][:, 768:1024].rearrange("p (a b) -> p a b", a=KC)
        lsr = p32[1][:, 0:128].rearrange("p (s a r) -> p s a r", s=2, a=KC)
        block_diag = p32[1][:, 128:256]
        rows = p32[1][0:1, 256:768].rearrange("o (i c) -> o i c", i=2)
        raw = {n: t[:].bitcast(F32).rearrange("p (a c) -> p a c", a=KC) for n, t in zip(raw_names, p_hi + p_lo)}
        o_sum = sb("o_sum", [P, NT, HEADS // 2, DH + 1])
        o_rec = sb("o_rec", [P, NT, HEADS // 2])
        y = sb("y", [P, NT, HEADS, DH])
        yT = [sb("yT_" + part, [P, KC, T], F32R) for part in ("hi", "lo")]
        ctx_sb = sb("ctx_sb", [M, C])
        ctxT = sb("ctxT", [P, KC, M])
        kxT = [sb(f"kxT{r}", [P, KC, M]) for r in range(RING)]
        vx = [sb(f"vx{r}", [M, C]) for r in range(RING)]
        x_res = sb("x_res", [P, NT, C])
        sum1 = sb("sum1", [P, NT, C])
        sum2 = sb("sum2", [P, NT, C])
        sum3 = sb("sum3", [P, NT, C])
        bn = [sb(f"bn{i}", [P, NT, 6]) for i in range(3)]
        mv = [sb(f"mv{i}", [P, NT, 2]) for i in range(3)]
        var = [sb(f"var{i}", [P, NT]) for i in range(3)]
        rstd = [sb(f"rstd{i}", [P, NT]) for i in range(3)]
        neg_mean = [sb(f"neg_mean{i}", [P, NT]) for i in range(3)]
        offset = [sb(f"offset{i}", [P, NT]) for i in range(3)]
        x1 = sum1
        x1p = sum1
        x1T = sb("x1T", [P, KC, T])
        s2_max = sb("s2_max", [P, NT])
        s2_neg = sb("s2_neg", [P, NT])
        s2_sum = sb("s2_sum", [P, NT])
        s2_rec = sb("s2_rec", [P, NT])
        a_exp = sb("a_exp", [P, NT, M])
        a_nrm = sb("a_nrm", [P, NT, M])
        g_sb = sb("g_sb", [M, C])
        x2 = sb("x2", [P, NT, C])
        x2T = sb("x2T", [P, KC, 1 + T])
        dx = sb("dx", [P, KC, T])
        xr = [sb("xr_" + part, [P, KC, T], F32R) for part in ("hi", "lo")]
        xk = [sb("xk_" + part, [P, KC, T], F32R) for part in ("hi", "lo")]
        k_act = [sb("k_act_" + part, [P, KC, T], F32R) for part in ("hi", "lo")]
        r_tanh = sb("r_tanh", [P, NT, C])
        gated = r_tanh
        xk_f32 = r_tanh[:].rearrange("p a b -> p (a b)").rearrange("p (a b) -> p a b", a=KC)
        xr_f32 = dx
        k_act_f32 = x1T
        x3 = sum3

        parts_dram = [[nc.dram_tensor(f"parts_dram{s}_{r}", [KC * P, 2, T], F32, kind="Internal").ap()
                       for r in range(RING)] for s in range(2)]

        ps_s = ps("ps_s", [P, 1024])
        ps_t = ps("ps_t", [P, 1024])
        ps_o = ps("ps_o", [P, NT, 512])
        ps_m = [ps(f"ps_m{i}", [P, 512]) for i in range(2)]

        setup_banks = [t for w in (ps_s, ps_t) for t in (w[:, 0:512], w[:, 512:1024])] + [ps_o[:, 0, :], ps_o[:, 1, :]]

        def sems(*names):
            return {n: sem(n) for n in names}

        filled = sems(*["f_" + n for n in ("xT", "q", "k", "v", "mT", "yT", "z1", "x1T", "s2", "g", "z2", "ctxT",
                                           "kx", "vx", "x2T", "k3", "r3", "v3")])
        s_filled, t_filled = sem("s_filled"), sem("t_filled")
        o_filled = [sem(f"o_filled{c}") for c in range(2)]
        exp_done = [sem(f"exp_done{c}") for c in range(6)]
        a_ = sems("xT_hi", "q_hi", "k_hi", "v_hi", "v_mid", "yT_hi", "x1T_ready", "a_exp_done", "g_ready",
                  "vx_ready", "x2T_ready", "k_relu_done", "r_tanh_done", "k_act_ready", "xk_hi", "xr_hi", "k_act_hi",
                  "ctxT_ready", "kxT_ready",
                  "x1_ready", "x2_ready")
        x3_ready = [sem(f"x3_ready{j}") for j in range(NT)]
        max_done = [sem(f"max_done{c}") for c in range(6)]
        p_hi_done = [sem(f"p_hi_done{c}") for c in range(6)]
        o_summed = [sem(f"o_summed{c}") for c in range(2)]
        o_inverse = [sem(f"o_inverse{c}") for c in range(2)]
        y_ready = [sem(f"y_ready{c}") for c in range(2)]
        v_ = sems("xT_lo", "yT_lo", "q_lo", "k_lo", "v_rest_done", "shift_done", "shift_hi", "shift_lo",
                  "s2_max_done", "s2_neg_done", "s2_rec_done", "a_ready", "sum1_done", "sum2_done", "sum3_done",
                  "gated_done", "xr_ready", "xk_ready", "xk_lo", "k_act_lo")
        bn_done = [sem(f"bn_done{i}") for i in range(3)]
        mv_done = [sem(f"mv_done{i}") for i in range(3)]
        p_lo_done = [sem(f"p_lo_done{c}") for c in range(6)]
        g_ = sems("x_c_ready", "x1p_ready", "v_lo", "dx_done", "xr_lo")
        var_done = [sem(f"var_done{i}") for i in range(3)]
        rstd_done = [sem(f"rstd_done{i}") for i in range(3)]
        neg_mean_done = [sem(f"neg_mean_done{i}") for i in range(3)]
        offset_done = [sem(f"offset_done{i}") for i in range(3)]
        x_loaded = sem("x_loaded")
        parts_saved = [[sem(f"parts_saved{s}_{r}") for r in range(RING)] for s in range(2)]
        stack_loaded = [sem(f"stack_loaded{r}") for r in range(RING)]
        shift_loaded = [sem(f"shift_loaded{r}") for r in range(RING)]
        ctx_loaded = sem("ctx_loaded")
        x_res_loaded = sem("x_res_loaded")
        out_saved = sem("out_saved")
        loaded_first, loaded_rest = sem("loaded_first"), sem("loaded_rest")
        raw_loaded = {n: (loaded_first, 16 * 2) if i < 2 else (loaded_rest, 16 * (len(raw_names) - 2))
                      for i, n in enumerate(raw_names)}
        lsr_loaded = sem("lsr_loaded")
        bias_loaded = sem("bias_loaded")
        small_loaded = sem("small_loaded")
        consts_ready = sem("consts_ready")
        consts_step = sem("consts_step")
        dve_consts = sem("dve_consts")
        ident_ready = sem("ident_ready")
        block_diag_ready = sem("block_diag_ready")
        v_zeroed = sem("v_zeroed")
        w_split = sem("w_split")
        setup_filled = sem("setup_filled")
        setup_taken = sem("setup_taken")

        def wait(eng, s, count):
            if not isinstance(count, int) or count > 0:
                eng.wait_ge(s, count)

        BANK_USERS = [
            [("xT", IN, v_["xT_lo"]), ("z1", CROSS, v_["sum1_done"]), ("x2T", FFN, a_["x2T_ready"]),
             ("x1T", CROSS, a_["x1T_ready"]), ("s2", CROSS, a_["a_exp_done"]), ("r3", FFN, a_["r_tanh_done"]),
             ("mT", SCORES, v_["shift_done"]), ("v3", FFN, v_["gated_done"]), ("kx", PROBS, a_["kxT_ready"])],
            [("yT", CROSS, v_["yT_lo"]), ("q", IN, v_["q_lo"]), ("k", IN, v_["k_lo"]),
             ("v", SCORES, v_["v_rest_done"]), ("k3", FFN, a_["k_relu_done"]), ("g", CROSS, a_["g_ready"]),
             ("ctxT", PROBS, a_["ctxT_ready"]), ("z2", CROSS, v_["sum2_done"]), ("vx", PROBS, a_["vx_ready"])],
        ]
        WHERE = {u[0]: (bank, i) for bank in range(2) for i, u in enumerate(BANK_USERS[bank])}

        def bank_of(what):
            return ps_m[WHERE[what][0]]

        def bank_free(pe, what, turn, at):
            bank, i = WHERE[what]
            users = BANK_USERS[bank]
            for back in range(1, 3 * len(users)):
                j = (i - back) % len(users)
                _, skew, read = users[j]
                at_j = at + (i - back - j) // len(users)
                b = Batch(turn, at_j, skew)
                if not b.static or 0 <= b.n < B:
                    pe.wait_ge(read, b.n + 1)
                    break
            return ps_m[bank]

        NARROW = (0, 1)
        S_ORDER = [0, 2, 3, 1, 4, 5]
        T_ORDER = [0, 2, 3, 1, 4, 5]

        def chunk_heads(c):
            return range(8 * c, 8 * c + 8) if c in NARROW else range(4 * (c - 2), 4 * (c - 2) + 4)

        def column(c, h):
            width = P if c in NARROW else T
            return 512 * (h % 2) + width * ((h - chunk_heads(c)[0]) // 2)

        def before(order, c, b):
            i = order.index(c)
            return (order[i - 1], b.n + 1) if i else (order[-1], b.n)

        block = es.enter_context(nc.Block())

        def flat(t):
            return t[:].rearrange("p a b -> p (a b)")

        def live(turn, at, skew):
            b = Batch(turn, at, skew)
            return not b.static or 0 <= b.n < B

        def run_steps(eng, step, ahead=0, late=0, between=None):
            first = LAST_SKEW + 1 + late
            loops = (B - first) // RING
            for t in range(first):
                step(t // RING, t % RING)
                if t == 0 and between:
                    between()
            q0, r0 = first // RING, first % RING
            with eng.Fori(q0, q0 + loops) as q:
                for u in range(RING):
                    step(q, r0 + u)
            for t in range(first + loops * RING, B + LAST_SKEW + ahead):
                step(t // RING, t % RING)

        @block.sync
        def _(sp):
            sp.dma_start(lsr[:, 0], Wq_lsr.rearrange("(a h) d r -> (h d) a r", a=KC)).then_inc(lsr_loaded, 16)
            sp.dma_start(lsr[:, 1], Wk_lsr.rearrange("(a h) d r -> (h d) a r", a=KC)).then_inc(lsr_loaded, 16)

            def load_weight(n):
                sp.dma_start(raw[n], raw_dram[n].rearrange("(a p) c -> p a c", p=P)).then_inc(raw_loaded[n][0], 16)

            def load_column(i, v, loaded):
                with nc.allow_non_contiguous_dma(reason="256 values to a column"):
                    sp.dma_start(cols[:, i, :], v.rearrange("(a p) -> p a", p=P)).then_inc(loaded, 16)

            for n in raw_names[:2]:
                load_weight(n)
            sp.dma_start(x_in[:], x[0, :, :].rearrange("(j p) c -> p j c", p=P)).then_inc(x_loaded, 16)
            load_column(BQ, bq, bias_loaded)
            load_column(BK, bk, bias_loaded)
            for n in raw_names[2:]:
                load_weight(n)
            for i, v in ((BV, bv), (MUR, mu_r), (MUK, mu_k)):
                load_column(i, v, small_loaded)
            for i, v in enumerate((bo, proj_b)):
                sp.dma_start(rows[:, i, :], v.rearrange("(o c) -> o c", o=1)).then_inc(small_loaded, 16)
            sp.dma_start(mask_i[:], mask_in.rearrange("(m o) -> m o", o=1)).then_inc(small_loaded, 16)

            def tokens(ap, n):
                return ap[n, :, :] if isinstance(n, int) else ap[bass.ds(n, 1), :, :].rearrange("o t c -> (o t) c")

            def load_x(b):
                wait(sp, filled["f_xT"], b.n)
                sp.dma_start(x_in[:], tokens(x, b.n).rearrange("(j p) c -> p j c", p=P)).then_inc(x_loaded, 16)

            def step(turn, at):
                if live(turn, at, IN) and not (isinstance(turn, int) and turn == at == 0):
                    load_x(Batch(turn, at, IN))
                at = at - 1
                b = Batch(turn, at, IN)
                if live(turn, at, PROBS):
                    c = Batch(turn, at, PROBS)
                    wait(sp, v_["sum1_done"], c.n)
                    sp.dma_start(x_res[:], tokens(x, c.n).rearrange("(j p) c -> p j c", p=P)).then_inc(x_res_loaded, 16)
                if live(turn, at, IN):
                    if b.static and b.n == 0:
                        sp.wait_ge(consts_ready, 1)
                    if not b.static or b.n >= 3:
                        before_it = Batch(turn, at - 3, IN)
                        sp.wait_ge(t_filled, before_it.chunks_done(T_ORDER, T_ORDER[-1]))
                    for s, ready, which in ((0, "q_lo", (0, 0, 1)), (1, "k_lo", (0, 1, 0))):
                        sp.wait_ge(v_[ready], b.n + 1)
                        sp.dma_start(parts_dram[s][b.slot].rearrange("(a p) w t -> p a w t", p=P), parts[s][:].bitcast(F32)) \
                            .then_inc(parts_saved[s][b.slot], 16)
                        sp.wait_ge(parts_saved[s][b.slot], b.dma_count(1))
                        for g in range(2):
                            for row, part in enumerate(which):
                                src = parts_dram[s][b.slot].rearrange("(j g d) w t -> g w d j t", g=2, d=DH)[g, part]
                                r0 = 64 * g + DH * row
                                sp.dma_start(stack[s][b.slot][r0:r0 + DH].bitcast(F32), src) \
                                    .then_inc(stack_loaded[b.slot], 16)
                if live(turn, at, SCORES):
                    c = Batch(turn, at, SCORES)
                    wait(sp, filled["f_ctxT"], c.n)
                    sp.dma_start(ctx_sb[:], tokens(ctx_in, c.n)).then_inc(ctx_loaded, 16)
                if live(turn, at, SCORES):
                    c = Batch(turn, at, SCORES)
                    sp.wait_ge(v_["shift_lo"], c.n + 1)
                    for g in range(2):
                        for part in range(2):
                            r0 = 64 * g + ONES_ROW + part
                            sp.dma_start(stack[0][c.slot][r0:r0 + 1].bitcast(F32),
                                         shift_parts[8 * g:8 * g + 8, part, :].bitcast(F32)).then_inc(shift_loaded[c.slot], 16)
                if live(turn, at, FFN):
                    c = Batch(turn, at, FFN)
                    for j in range(NT):
                        sp.wait_ge(x3_ready[j], c.n + 1)
                        sp.dma_start(tokens(out, c.n)[j * P:(j + 1) * P, :], x3[:, j, :]).then_inc(out_saved, 16)

            run_steps(sp, step, ahead=1)
            sp.wait_ge(out_saved, 16 * NT * B)

        @block.tensor
        def _(pe):
            bank_no = [0]

            def setup_bank():
                n = bank_no[0]
                bank_no[0] += 1
                if n >= len(setup_banks):
                    pe.wait_ge(setup_taken, n + 1 - len(setup_banks))
                return setup_banks[n % len(setup_banks)]

            pe.wait_ge(ident_ready, 1)
            pe.wait_ge(lsr_loaded, 32)
            bank = setup_bank()
            for s in range(2):
                for a in range(KC):
                    i = s * KC + a
                    last = nc.tensor.transpose(bank[0:RANK, i * P:(i + 1) * P], lsr[:, s, a, :], ident[:])
            last.then_inc(setup_filled, 1)

            def turn_weight(n):
                bank = setup_bank()
                pe.wait_ge(*raw_loaded[n])
                for k in range(KC):
                    for a in range(KC):
                        last = nc.tensor.transpose(bank[:, k * C + a * P:k * C + (a + 1) * P],
                                                   raw[n][:, a, k * P:(k + 1) * P], ident[:])
                last.then_inc(setup_filled, 1)

            turn_weight("Wk")
            bank = setup_bank()
            pe.wait_ge(setup_taken, 1)
            for a in range(KC):
                last = nc.tensor.matmul(bank[:, a * P:(a + 1) * P], lsrT[:, 0, a, :], lsrT[:, 1, a, :],
                                        start=True, stop=True)
            last.then_inc(setup_filled, 1)
            pe.wait_ge(*raw_loaded["Wq"])
            pe.wait_ge(bias_loaded, 16 * 2)
            bank = setup_bank()
            pe.wait_ge(setup_taken, 3)
            for k in range(KC):
                for a in range(KC):
                    last = nc.tensor.matmul(bank[:, k * C + a * P:k * C + (a + 1) * P],
                                            raw["Wq"][:, a, k * P:(k + 1) * P], lsr_prod[:, a, :], start=True, stop=True)
            last.then_inc(setup_filled, 1)
            bank = setup_bank()
            for a in range(KC):
                last = nc.tensor.matmul(bank[:, a:a + 1], lsr_prod[:, a, :], cols[:, BQ, a:a + 1], start=True, stop=True)
            last.then_inc(setup_filled, 1)
            pe.wait_ge(setup_taken, SETUP_FIRST)

            def other_weights():
                for n in turned_names[1:]:
                    turn_weight(n)
                for n in ("Wxq", "Wxk"):
                    pe.wait_ge(*raw_loaded[n])
                bank = setup_bank()
                for k in range(KC):
                    for a in range(KC):
                        last = nc.tensor.matmul(bank[:, k * C:(k + 1) * C], raw["Wxk"][:, a, k * P:(k + 1) * P],
                                                raw["Wxq"][:, a, :], start=(a == 0), stop=(a == KC - 1))
                last.then_inc(setup_filled, 1)
                bank = setup_bank()
                pe.wait_ge(dve_consts, 1)
                pe.wait_ge(consts_ready, 1)
                pe.wait_ge(setup_taken, 7)
                for a in range(KC):
                    for e, part in enumerate((w_hi["Wo"], w_lo["Wo"])):
                        nc.tensor.matmul(bank[:, 0:C], bv_rep[:, a, :], part[:, a, :].bitcast(F32),
                                         start=(a == 0 and e == 0), stop=False)
                nc.tensor.matmul(bank[:, 0:C], ones_row[:], rows[:, 0, :], start=False, stop=True).then_inc(setup_filled, 1)
                bank = setup_bank()
                nc.tensor.matmul(bank[:, 0:C], ones_row[:], rows[:, 1, :], start=True, stop=True).then_inc(setup_filled, 1)
                assert bank_no[0] == SETUP_TOTAL
                pe.wait_ge(setup_taken, SETUP_TOTAL)

            def turn_tiles(bank, src):
                for k in range(KC):
                    for j in range(NT):
                        last = nc.tensor.transpose(bank[:, k * T + j * P:k * T + (j + 1) * P],
                                                   src[:, j, k * P:(k + 1) * P], ident[:])
                return last

            def rows_out(bank, w, src):
                n = src.shape[-1]
                for a in range(KC):
                    for k in range(KC):
                        last = nc.tensor.matmul(bank[:, a * n:(a + 1) * n], w[:, k, a * P:(a + 1) * P], src[:, k, :],
                                                start=(k == 0), stop=(k == KC - 1))
                return last

            def tokens_out(bank, src, w, tiles=NT, rows=P):
                for j in range(tiles):
                    for k in range(KC):
                        last = nc.tensor.matmul(bank[0:rows, j * C:(j + 1) * C], src[:, k, j * P:j * P + rows], w[:, k, :],
                                                start=(k == 0), stop=(k == KC - 1))
                return last

            def split_terms(w, src):
                return [(w_hi[w], src[0]), (w_hi[w], src[1]), (w_lo[w], src[0])]

            def rows_out_split(bank, w, src):
                for a in range(KC):
                    terms = [(ww[:, k, a * P:(a + 1) * P], ss[:, k, :]) for k in range(KC) for ww, ss in split_terms(w, src)]
                    for e, (ww, ss) in enumerate(terms):
                        last = nc.tensor.matmul(bank[:, a * T:(a + 1) * T], ww, ss, start=(e == 0),
                                                stop=(e == len(terms) - 1))
                return last

            def tokens_out_split(bank, src, w):
                for j in range(NT):
                    terms = [(ss[:, k, j * P:(j + 1) * P], ww[:, k, :]) for k in range(KC) for ww, ss in split_terms(w, src)]
                    for e, (ss, ww) in enumerate(terms):
                        last = nc.tensor.matmul(bank[:, j * C:(j + 1) * C], ss, ww, start=(e == 0),
                                                stop=(e == len(terms) - 1))
                return last

            def scores(b, c, target, free, free_count, done, left, right, mask):
                wait(pe, free, free_count)
                heads = chunk_heads(c)
                rows_at = 0 if (c in NARROW) == (left is stack[0]) else P
                width, col = (P, rows_at) if c in NARROW else (T, 0)
                for h in heads:
                    r0 = 64 * (h % 2)
                    at_h = column(c, h)
                    o = target[:, at_h:at_h + width]
                    first_in_bank = h - heads[0] < 2
                    rows_n = STACK_ROWS if left is stack[1] else ONES_ROW
                    nc.tensor.matmul(o, left[b.slot][r0:r0 + rows_n, h // 2, rows_at:rows_at + P],
                                     right[b.slot][r0:r0 + rows_n, h // 2, col:col + width],
                                     start=first_in_bank, stop=False, skip_group_check=True)
                for half in range(2):
                    o = target[:, half * 512:(half + 1) * 512]
                    if c in NARROW:
                        last = nc.tensor.matmul(o, identb[:], mask[:].rearrange("p a b -> p (a b)"),
                                                start=False, stop=True, skip_group_check=True)
                    else:
                        o = o.rearrange("p (n w) -> p n w", n=2)
                        o = o[:, :, P:2 * P] if left is stack[0] else o[:, :, 0:P]
                        last = nc.tensor.matmul(o, identb[:], mask[:, 0:2, :], start=False, stop=True,
                                                skip_group_check=True)
                last.then_inc(done, 1)

            def step(turn, at):
                A, Sb, Pb, X, F = (Batch(turn, at, s) for s in range(5))
                on = [live(turn, at, s) for s in range(5)]

                def S(c):
                    if on[SCORES]:
                        if c == S_ORDER[0]:
                            pe.wait_ge(stack_loaded[Sb.slot], Sb.dma_count(12))
                        prev, count = before(S_ORDER, c, Sb)
                        scores(Sb, c, ps_s, max_done[prev], count, s_filled, stack[0], stack[1], mask_s)

                def Tr(c):
                    if on[PROBS]:
                        if c == T_ORDER[0]:
                            pe.wait_ge(shift_loaded[Pb.slot], Pb.dma_count(4))
                        prev, count = before(T_ORDER, c, Pb)
                        scores(Pb, c, ps_t, exp_done[prev], count, t_filled, stack[1], stack[0], mask_t)

                def PV(half):
                    if not on[PROBS]:
                        return
                    b = Pb
                    wait(pe, o_summed[1 - half], 2 * (b.n + half))
                    if half == 0:
                        pe.wait_ge(g_["v_lo"], b.n + 1)
                    for c in (half, 2 + 2 * half, 3 + 2 * half):
                        pe.wait_ge(p_lo_done[c], b.n + 1)
                    for h8 in range(8):
                        h = 8 * half + h8
                        w = 2 + h // 4
                        cw, cn = column(w, h), column(half, h)
                        v = [v_parts[b.slot][:, j, h].rearrange("p a d -> p (a d)") for j in range(2)]
                        n = v[0].shape[-1]
                        for i in range(NT):
                            o = ps_o[:, i, h8 * n:(h8 + 1) * n]
                            terms = [(p[w][:, cw + i * P:cw + (i + 1) * P], v[0]) for p in (p_hi, p_lo)]
                            if i == 1:
                                terms += [(p[half][:, cn:cn + P], v[1]) for p in (p_hi, p_lo)]
                            for e, (p, vv) in enumerate(terms):
                                last = nc.tensor.matmul(o, p, vv, start=(e == 0), stop=(e == len(terms) - 1),
                                                        skip_group_check=True)
                    last.then_inc(o_filled[half], 1)

                if on[IN]:
                    bank = bank_free(pe, "xT", turn, at)
                    pe.wait_ge(x_loaded, (A.n + 1) * 16)
                    turn_tiles(bank, x_in).then_inc(filled["f_xT"], 1)
                S(0)
                if on[CROSS]:
                    bank = bank_free(pe, "yT", turn, at)
                    pe.wait_ge(y_ready[1], X.n + 1)
                    turn_tiles(bank, y[:].rearrange("p j h d -> p j (h d)")).then_inc(filled["f_yT"], 1)
                Tr(0)
                S(2)
                if on[IN]:
                    bank = bank_free(pe, "q", turn, at)
                    pe.wait_ge(v_["xT_lo"], A.n + 1)
                    rows_out_split(bank, "Wq", xT[A.slot]).then_inc(filled["f_q"], 1)
                Tr(2)
                if on[CROSS]:
                    bank = bank_free(pe, "z1", turn, at)
                    pe.wait_ge(v_["yT_lo"], X.n + 1)
                    tokens_out_split(bank, yT, "Wo").then_inc(filled["f_z1"], 1)
                S(3)
                Tr(3)
                if on[FFN]:
                    bank = bank_free(pe, "x2T", turn, at)
                    pe.wait_ge(a_["x2_ready"], F.n + 1)
                    turn_tiles(bank, x2).then_inc(filled["f_x2T"], 1)
                if on[IN]:
                    bank = bank_free(pe, "k", turn, at)
                    rows_out_split(bank, "Wk", xT[A.slot]).then_inc(filled["f_k"], 1)
                S(1)
                Tr(1)
                if on[CROSS]:
                    bank = bank_free(pe, "x1T", turn, at)
                    pe.wait_ge(a_["x1_ready"], X.n + 1)
                    turn_tiles(bank, x1).then_inc(filled["f_x1T"], 1)
                if on[SCORES]:
                    bank = bank_free(pe, "v", turn, at)
                    pe.wait_ge(v_["xT_lo"], Sb.n + 1)
                    tokens_out_split(bank, xT[Sb.slot], "Wv").then_inc(filled["f_v"], 1)
                S(4)
                Tr(4)
                if on[CROSS]:
                    bank = bank_free(pe, "s2", turn, at)
                    pe.wait_ge(a_["x1T_ready"], X.n + 1)
                    pe.wait_ge(a_["kxT_ready"], X.n + 1)
                    for j in range(NT):
                        for k in range(KC):
                            last = nc.tensor.matmul(bank[:, j * M:(j + 1) * M], x1T[:, k, j * P:(j + 1) * P],
                                                    kxT[X.slot][:, k, :], start=(k == 0), stop=(k == KC - 1))
                    last.then_inc(filled["f_s2"], 1)
                if on[FFN]:
                    bank = bank_free(pe, "k3", turn, at)
                    pe.wait_ge(v_["xk_lo"], F.n + 1)
                    rows_out_split(bank, "Wkf", xk).then_inc(filled["f_k3"], 1)
                S(5)
                Tr(5)
                if on[FFN]:
                    bank = bank_free(pe, "r3", turn, at)
                    pe.wait_ge(g_["xr_lo"], F.n + 1)
                    tokens_out_split(bank, xr, "Wr").then_inc(filled["f_r3"], 1)
                if on[CROSS]:
                    bank = bank_free(pe, "g", turn, at)
                    pe.wait_ge(v_["a_ready"], X.n + 1)
                    for k in range(KC):
                        last = nc.tensor.matmul(bank[0:M, 0:C], a_nrm[:, k, :], wT["Wp"][:, k, :],
                                                start=(k == 0), stop=(k == KC - 1))
                    last.then_inc(filled["f_g"], 1)
                if on[SCORES]:
                    bank = bank_free(pe, "mT", turn, at)
                    pe.wait_ge(max_done[5], Sb.n + 1)
                    for i in range(NT):
                        last = nc.tensor.transpose(bank[0:HEADS, i * P:(i + 1) * P],
                                                   row_max[:, i].rearrange("p g j -> p (g j)"), ident[:])
                    last.then_inc(filled["f_mT"], 1)
                PV(0)
                if on[PROBS]:
                    bank = bank_free(pe, "ctxT", turn, at)
                    pe.wait_ge(ctx_loaded, (Pb.n + 1) * 16)
                    for k in range(KC):
                        last = nc.tensor.transpose(bank[:, k * M:(k + 1) * M], ctx_sb[:, k * P:(k + 1) * P],
                                                   ident[0:M, 0:M])
                    last.then_inc(filled["f_ctxT"], 1)
                if on[FFN]:
                    bank = bank_free(pe, "v3", turn, at)
                    pe.wait_ge(v_["k_act_lo"], F.n + 1)
                    tokens_out_split(bank, k_act, "Wvf").then_inc(filled["f_v3"], 1)
                if on[CROSS]:
                    bank = bank_free(pe, "z2", turn, at)
                    pe.wait_ge(a_["g_ready"], X.n + 1)
                    pe.wait_ge(a_["vx_ready"], X.n + 1)
                    for j in range(NT):
                        last = nc.tensor.matmul(bank[:, j * C:(j + 1) * C], vx[X.slot][:, j * P:(j + 1) * P], g_sb[:],
                                                start=True, stop=True)
                    last.then_inc(filled["f_z2"], 1)
                PV(1)
                if on[PROBS]:
                    bank = bank_free(pe, "kx", turn, at)
                    pe.wait_ge(a_["ctxT_ready"], Pb.n + 1)
                    rows_out(bank, wx_fold, ctxT).then_inc(filled["f_kx"], 1)
                if on[PROBS]:
                    bank = bank_free(pe, "vx", turn, at)
                    tokens_out(bank, ctxT, wT["Wxv"], tiles=1, rows=M).then_inc(filled["f_vx"], 1)

            run_steps(pe, step, between=other_weights)

        @block.scalar
        def _(act):
            def step(turn, at):
                A, Sb, Pb, X, F = (Batch(turn, at, s) for s in range(5))
                on = [live(turn, at, s) for s in range(5)]

                def exp(c):
                    if not on[PROBS]:
                        return
                    i = T_ORDER.index(c)
                    act.wait_ge(t_filled, Pb.chunks_done(T_ORDER, c))
                    prev, count = (T_ORDER[i - 3], Pb.n + 1) if i >= 3 else (T_ORDER[i + 3], Pb.n)
                    wait(act, p_lo_done[prev], count)
                    nc.scalar.activation(p32[i % 3][:], ps_t[:], ACT.Exp).then_inc(exp_done[c], 1)

                def split_hi(b, s, name, bias, what):
                    act.wait_ge(filled["f_" + what], b.n + 1)
                    prev = Batch(turn, at - 1, IN)
                    if not prev.static or prev.n >= 0:
                        act.wait_ge(parts_saved[s][prev.slot], prev.dma_count(1))
                    bank = ps_m[WHERE[what][0]]
                    for a in range(KC):
                        last = nc.scalar.activation(parts[s][:, a, 0, :], bank[:, a * T:(a + 1) * T], ACT.Identity,
                                                    bias=bias[a])
                    last.then_inc(a_[name], 1)

                def normalise(i, b, dst, src, done):
                    act.wait_ge(offset_done[i], b.n + 1)
                    for j in range(NT):
                        last = nc.scalar.activation(dst[:, j, :], src[:, j, :], ACT.Identity, bias=offset[i][:, j:j + 1],
                                                    scale=rstd[i][:, j:j + 1])
                    last.then_inc(a_[done], 1)

                def copy_high(c):
                    if on[PROBS]:
                        act.wait_ge(exp_done[c], Pb.n + 1)
                        wait(act, o_filled[1], Pb.n)
                        nc.scalar.copy(p_hi[c][:], p32[T_ORDER.index(c) % 3][:]).then_inc(p_hi_done[c], 1)

                if on[IN]:
                    act.wait_ge(filled["f_xT"], A.n + 1)
                    wait(act, filled["f_v"], A.n - 2)
                    nc.scalar.copy(flat(xT[A.slot][0]), bank_of("xT")[:]).then_inc(a_["xT_hi"], 1)
                if on[CROSS]:
                    act.wait_ge(filled["f_yT"], X.n + 1)
                    wait(act, filled["f_z1"], X.n)
                    nc.scalar.copy(flat(yT[0]), bank_of("yT")[:]).then_inc(a_["yT_hi"], 1)
                X1, F1 = Batch(turn, at - 1, CROSS), Batch(turn, at - 1, FFN)
                exp(0)
                if live(turn, at - 1, CROSS):
                    wait(act, v_["sum3_done"], X1.n)
                    normalise(1, X1, x2, sum2, "x2_ready")
                if on[IN]:
                    split_hi(A, 0, "q_hi", [bq_fold[:, a:a + 1] for a in range(KC)], "q")
                exp(2)
                if live(turn, at - 1, FFN):
                    act.wait_ge(offset_done[2], F1.n + 1)
                    for j in range(NT):
                        nc.scalar.activation(x3[:, j, :], sum3[:, j, :], ACT.Identity, bias=offset[2][:, j:j + 1],
                                             scale=rstd[2][:, j:j + 1]).then_inc(x3_ready[j], 1)
                if on[FFN]:
                    act.wait_ge(filled["f_x2T"], F.n + 1)
                    wait(act, v_["xr_ready"], F.n)
                    nc.scalar.copy(x2T[:, :, 1:1 + T], bank_of("x2T")[:].rearrange("p (a b) -> p a b", a=KC)) \
                        .then_inc(a_["x2T_ready"], 1)
                exp(3)
                if on[IN]:
                    split_hi(A, 1, "k_hi", [cols[:, BK, a:a + 1] for a in range(KC)], "k")
                if on[CROSS]:
                    wait(act, filled["f_x1T"], X.n)
                    normalise(0, X, x1, sum1, "x1_ready")
                exp(1)
                if on[FFN]:
                    act.wait_ge(v_["xk_ready"], F.n + 1)
                    wait(act, filled["f_k3"], F.n)
                    nc.scalar.copy(xk[0][:], xk_f32).then_inc(a_["xk_hi"], 1)
                if on[CROSS]:
                    act.wait_ge(filled["f_x1T"], X.n + 1)
                    wait(act, filled["f_s2"], X.n)
                    wait(act, v_["k_act_lo"], F.n)
                    nc.scalar.copy(flat(x1T), bank_of("x1T")[:]).then_inc(a_["x1T_ready"], 1)
                if on[SCORES]:
                    act.wait_ge(filled["f_v"], Sb.n + 1)
                    wait(act, o_filled[1], Sb.n - 2)
                    for j in range(NT):
                        last = nc.scalar.copy(v_parts[Sb.slot][:, j, :, 0, 0:DH],
                                              bank_of("v")[:, j * C:(j + 1) * C].rearrange("p (h d) -> p h d", h=HEADS))
                    last.then_inc(a_["v_hi"], 1)
                if on[FFN]:
                    act.wait_ge(v_["xr_ready"], F.n + 1)
                    wait(act, filled["f_r3"], F.n)
                    nc.scalar.copy(flat(xr[0]), flat(xr_f32)).then_inc(a_["xr_hi"], 1)
                exp(4)
                copy_high(4)
                if on[CROSS]:
                    act.wait_ge(v_["s2_neg_done"], X.n + 1)
                    wait(act, v_["a_ready"], X.n)
                    for j in range(NT):
                        last = nc.scalar.activation(a_exp[:, j, :], bank_of("s2")[:, j * M:(j + 1) * M], ACT.Exp,
                                                    bias=s2_neg[:, j:j + 1], scale=XSCALE, accum_out=s2_sum[:, j:j + 1])
                    last.then_inc(a_["a_exp_done"], 1)
                if on[FFN]:
                    act.wait_ge(filled["f_k3"], F.n + 1)
                    wait(act, filled["f_v3"], F.n)
                    nc.scalar.activation(flat(k_act_f32), bank_of("k3")[:], ACT.Relu).then_inc(a_["k_relu_done"], 1)
                if on[FFN]:
                    act.wait_ge(a_["k_relu_done"], F.n + 1)
                    nc.scalar.activation(flat(k_act_f32), flat(k_act_f32), ACT.Square) \
                        .then_inc(a_["k_act_ready"], 1)
                exp(5)
                if on[FFN]:
                    act.wait_ge(filled["f_r3"], F.n + 1)
                    wait(act, v_["sum3_done"], F.n)
                    nc.scalar.activation(flat(r_tanh), bank_of("r3")[:], ACT.Tanh, scale=0.5) \
                        .then_inc(a_["r_tanh_done"], 1)
                if on[FFN]:
                    act.wait_ge(a_["k_act_ready"], F.n + 1)
                    wait(act, filled["f_v3"], F.n)
                    nc.scalar.copy(flat(k_act[0]), flat(k_act_f32)).then_inc(a_["k_act_hi"], 1)
                if on[CROSS]:
                    act.wait_ge(filled["f_g"], X.n + 1)
                    wait(act, filled["f_z2"], X.n)
                    nc.scalar.activation(g_sb[:], bank_of("g")[0:M, 0:C], ACT.Copy, scale=keep[:]) \
                        .then_inc(a_["g_ready"], 1)
                copy_high(5)
                if on[SCORES]:
                    act.wait_ge(v_["v_rest_done"], Sb.n + 1)
                    for j in range(NT):
                        last = nc.scalar.copy(v_parts[Sb.slot][:, j, :, 1, 0:DH],
                                              v_rest[:, j, :].rearrange("p (h d) -> p h d", h=HEADS))
                    last.then_inc(a_["v_mid"], 1)
                if on[PROBS]:
                    act.wait_ge(filled["f_ctxT"], Pb.n + 1)
                    wait(act, filled["f_vx"], Pb.n)
                    nc.scalar.copy(flat(ctxT), bank_of("ctxT")[:, 0:KC * M]).then_inc(a_["ctxT_ready"], 1)
                    act.wait_ge(filled["f_kx"], Pb.n + 1)
                    wait(act, filled["f_s2"], Pb.n - 2)
                    nc.scalar.copy(flat(kxT[Pb.slot]), bank_of("kx")[:, 0:KC * M]).then_inc(a_["kxT_ready"], 1)
                if on[PROBS]:
                    act.wait_ge(filled["f_vx"], Pb.n + 1)
                    wait(act, filled["f_z2"], Pb.n - 2)
                    nc.scalar.copy(vx[Pb.slot][:], bank_of("vx")[0:M, 0:C]).then_inc(a_["vx_ready"], 1)

            act.wait_ge(setup_taken, SETUP_FIRST)
            run_steps(act, step, ahead=1)

        @block.vector
        def _(dve):
            taken, splits = [0], [0]

            def setup_take():
                n = taken[0]
                dve.wait_ge(setup_filled, n + 1)
                taken[0] += 1
                return setup_banks[n % len(setup_banks)]

            def split_bank(n):
                bank = setup_take()
                nc.vector.tensor_copy(flat(w_hi[n]), bank).then_inc(w_split, 1)
                splits[0] += 1
                dve.wait_ge(w_split, splits[0])
                nc.vector.tensor_tensor(flat(w_lo[n]), bank, flat(w_hi[n]).bitcast(F32), ALU.subtract) \
                    .then_inc(setup_taken, 1)

            def copy_bank(dst):
                bank = setup_take()
                nc.vector.tensor_copy(dst, bank[:, 0:dst.shape[-1]]).then_inc(setup_taken, 1)

            for r in range(RING):
                nc.vector.memset(v_parts[r][:, :, :, :, DH:DH + 1], 0.0).then_inc(v_zeroed, 1)
            dve.wait_ge(v_zeroed, RING)
            for r in range(RING):
                nc.vector.memset(v_parts[r][:, :, :, 0, DH:DH + 1], 1.0).then_inc(v_zeroed, 1)
            dve.wait_ge(ident_ready, 1)
            bank = setup_take()
            nc.vector.tensor_copy(p32[0][0:RANK, 0:512], bank[0:RANK, :]).then_inc(setup_taken, 1)
            split_bank("Wk")
            bank = setup_take()
            dve.wait_ge(block_diag_ready, 1)
            for a in range(KC):
                last = nc.vector.scalar_tensor_tensor(lsr_prod[:, a, :], bank[:, a * P:(a + 1) * P], float(RANK) ** -0.5,
                                                      block_diag, op0=ALU.mult, op1=ALU.mult)
            last.then_inc(setup_taken, 1)
            split_bank("Wq")
            copy_bank(bq_fold[:])
            assert taken[0] == SETUP_FIRST
            dve.wait_ge(setup_taken, SETUP_FIRST)

            def other_weights():
                dve.wait_ge(small_loaded, 16 * 6)
                nc.vector.tensor_scalar(keep[:], mask_i[:], 0.0, None, ALU.not_equal)
                for a in range(KC):
                    last = nc.vector.tensor_scalar(bv_rep[:, a, :], ident[:], 0.0, cols[:, BV, a:a + 1], ALU.mult, ALU.add)
                last.then_inc(dve_consts, 1)
                for n in turned_names[1:]:
                    if n in SPLIT:
                        split_bank(n)
                    else:
                        copy_bank(flat(wT[n]))
                copy_bank(flat(wx_fold))
                copy_bank(c1[:])
                copy_bank(pb_rep[:])
                assert taken[0] == SETUP_TOTAL
                dve.wait_ge(setup_taken, SETUP_TOTAL)
                dve.wait_ge(consts_ready, 1)

            def step(turn, at):
                A, Sb, Pb, X, F = (Batch(turn, at, s) for s in range(5))
                on = [live(turn, at, s) for s in range(5)]

                def row_maxima(c):
                    if not on[SCORES]:
                        return
                    dve.wait_ge(s_filled, Sb.chunks_done(S_ORDER, c))
                    if c == S_ORDER[0]:
                        wait(dve, filled["f_mT"], Sb.n)
                    heads = chunk_heads(c)
                    tile = 0 if c in NARROW else 1
                    j0, nj = heads[0] // 2, len(heads) // 2
                    nc.vector.tensor_reduce(row_max[:, tile, :, j0:j0 + nj],
                                            ps_s[:].rearrange("p (g j w) -> p g j w", j=nj, g=2), AX_X, ALU.max) \
                        .then_inc(max_done[c], 1)

                def high_part(c):
                    if not on[PROBS]:
                        return
                    dve.wait_ge(exp_done[c], Pb.n + 1)
                    half = c if c in NARROW else (c - 2) // 2
                    wait(dve, o_filled[half], Pb.n)
                    nc.vector.tensor_copy(p_hi[c][:], p32[T_ORDER.index(c) % 3][:]).then_inc(p_hi_done[c], 1)

                def split_lo(b, s, hi, lo, bias, what):
                    dve.wait_ge(a_[hi], b.n + 1)
                    bank = ps_m[WHERE[what][0]]
                    for a in range(KC):
                        last = nc.vector.scalar_tensor_tensor(parts[s][:, a, 1, :], bank[:, a * T:(a + 1) * T], bias[a],
                                                              parts[s][:, a, 0, :].bitcast(F32),
                                                              op0=ALU.add, op1=ALU.subtract)
                    last.then_inc(v_[lo], 1)

                def stats(i, b, src, summed):
                    dve.wait_ge(summed, b.n + 1)
                    wait(dve, mv_done[i], b.n)
                    for j in range(NT):
                        last = nc.vector.bn_stats(bn[i][:, j, :], src[:, j, :])
                    last.then_inc(bn_done[i], 1)
                    dve.wait_ge(bn_done[i], b.n + 1)
                    wait(dve, offset_done[i], b.n)
                    nc.vector.memset(pause[:], 0.0)
                    for j in range(NT):
                        last = nc.vector.bn_aggr(mv[i][:, j, :], bn[i][:, j, :])
                    last.then_inc(mv_done[i], 1)

                def attention_sums(half):
                    if not on[PROBS]:
                        return
                    b = Pb
                    dve.wait_ge(o_filled[half], b.n + 1)
                    wait(dve, y_ready[1 - half], b.n + half)
                    for i in range(NT):
                        nc.vector.tensor_reduce(o_sum[:, i],
                                                ps_o[:, i, 0:8 * 3 * (DH + 1)].rearrange("p (h a d) -> p h d a", h=8, a=3),
                                                AX_X, ALU.add).then_inc(o_summed[half], 1)
                    dve.wait_ge(o_summed[half], (b.n + 1) * 2)
                    nc.vector.reciprocal(o_rec[:], o_sum[:, :, :, DH]).then_inc(o_inverse[half], 1)

                def attention_out(half):
                    if not on[PROBS]:
                        return
                    b = Pb
                    dve.wait_ge(o_inverse[half], b.n + 1)
                    wait(dve, filled["f_yT"], b.n)
                    for i in range(NT):
                        last = nc.vector.tensor_tensor(y[:, i, 8 * half:8 * half + 8, :], o_sum[:, i, :, 0:DH],
                                                       o_rec[:, i, :].unsqueeze(2).to_broadcast([P, 8, DH]), ALU.mult)
                    last.then_inc(y_ready[half], 1)

                def mix(dst, mu, ready):
                    for k in range(KC):
                        last = nc.vector.scalar_tensor_tensor(dst[:, k, :], dx[:, k, :], cols[:, mu, k:k + 1],
                                                              x2T[:, k, 0:T], op0=ALU.mult, op1=ALU.add)
                    last.then_inc(v_[ready], 1)

                def low_of(value, t, hi, lo):
                    dve.wait_ge(a_[hi], F.n + 1)
                    nc.vector.tensor_tensor(t[1][:], value[:], t[0][:].bitcast(F32), ALU.subtract).then_inc(v_[lo], 1)

                def turned_lo(b, what, dst, used):
                    dve.wait_ge(a_[what + "_hi"], b.n + 1)
                    wait(dve, *used)
                    nc.vector.tensor_tensor(flat(dst[1]), bank_of(what)[:], flat(dst[0]).bitcast(F32), ALU.subtract) \
                        .then_inc(v_[what + "_lo"], 1)

                if on[IN]:
                    turned_lo(A, "xT", xT[A.slot], (filled["f_v"], A.n - 2))
                row_maxima(0)
                if on[CROSS]:
                    turned_lo(X, "yT", yT, (filled["f_z1"], X.n))
                if live(turn, at - 1, FFN):
                    stats(2, Batch(turn, at - 1, FFN), sum3, v_["sum3_done"])
                high_part(0)
                row_maxima(2)
                if on[IN]:
                    split_lo(A, 0, "q_hi", "q_lo", [bq_fold[:, a:a + 1] for a in range(KC)], "q")
                if on[CROSS]:
                    dve.wait_ge(filled["f_z1"], X.n + 1)
                    dve.wait_ge(g_["x_c_ready"], X.n + 1)
                    wait(dve, a_["x1_ready"], X.n)
                    nc.vector.tensor_tensor(flat(sum1), bank_of("z1")[:], flat(x_res), ALU.add) \
                        .then_inc(v_["sum1_done"], 1)
                if on[CROSS]:
                    stats(0, X, sum1, v_["sum1_done"])
                row_maxima(3)
                high_part(2)
                high_part(3)
                if on[IN]:
                    split_lo(A, 1, "k_hi", "k_lo", [cols[:, BK, a:a + 1] for a in range(KC)], "k")
                if on[FFN]:
                    dve.wait_ge(g_["dx_done"], F.n + 1)
                    mix(xk_f32, MUK, "xk_ready")
                row_maxima(1)
                if on[FFN]:
                    mix(xr_f32, MUR, "xr_ready")
                    low_of(xk_f32, xk, "xk_hi", "xk_lo")
                if on[SCORES]:
                    dve.wait_ge(a_["v_hi"], Sb.n + 1)
                    wait(dve, g_["v_lo"], Sb.n)
                    for j in range(NT):
                        last = nc.vector.tensor_tensor(
                            v_rest[:, j, :].rearrange("p (h d) -> p h d", h=HEADS),
                            bank_of("v")[:, j * C:(j + 1) * C].rearrange("p (h d) -> p h d", h=HEADS),
                            v_parts[Sb.slot][:, j, :, 0, 0:DH], ALU.subtract)
                    last.then_inc(v_["v_rest_done"], 1)
                row_maxima(4)
                if on[CROSS]:
                    dve.wait_ge(filled["f_s2"], X.n + 1)
                    wait(dve, v_["s2_neg_done"], X.n)
                    nc.vector.tensor_reduce(s2_max[:], bank_of("s2")[:, 0:NT * M].rearrange("p (j m) -> p j m", j=NT),
                                            AX_X, ALU.max).then_inc(v_["s2_max_done"], 1)
                    dve.wait_ge(v_["s2_max_done"], X.n + 1)
                    wait(dve, a_["a_exp_done"], X.n)
                    nc.vector.tensor_scalar(s2_neg[:], s2_max[:], -XSCALE, None, ALU.mult) \
                        .then_inc(v_["s2_neg_done"], 1)
                high_part(1)
                if on[CROSS]:
                    dve.wait_ge(a_["a_exp_done"], X.n + 1)
                    wait(dve, v_["a_ready"], X.n)
                    nc.vector.reciprocal(s2_rec[:], s2_sum[:]).then_inc(v_["s2_rec_done"], 1)
                    dve.wait_ge(v_["s2_rec_done"], X.n + 1)
                    wait(dve, filled["f_g"], X.n)
                    for j in range(NT):
                        last = nc.vector.tensor_scalar(a_nrm[:, j, :], a_exp[:, j, :], s2_rec[:, j:j + 1], None, ALU.mult)
                    last.then_inc(v_["a_ready"], 1)
                row_maxima(5)
                if on[SCORES]:
                    dve.wait_ge(filled["f_mT"], Sb.n + 1)
                    prev = Batch(turn, at - 1, SCORES)
                    if not prev.static or prev.n >= 0:
                        dve.wait_ge(shift_loaded[prev.slot], prev.dma_count(4))
                    nc.vector.tensor_scalar(shift, bank_of("mT")[0:HEADS, 0:T], -1.0, LN2_12, ALU.mult, ALU.add) \
                        .then_inc(v_["shift_done"], 1)
                if on[FFN]:
                    low_of(k_act_f32, k_act, "k_act_hi", "k_act_lo")
                if on[SCORES]:
                    dve.wait_ge(v_["shift_done"], Sb.n + 1)
                    nc.vector.tensor_copy(shift_parts[:, 0, :], shift).then_inc(v_["shift_hi"], 1)
                    dve.wait_ge(v_["shift_hi"], Sb.n + 1)
                    nc.vector.tensor_tensor(shift_parts[:, 1, :], shift, shift_parts[:, 0, :].bitcast(F32),
                                            ALU.subtract).then_inc(v_["shift_lo"], 1)
                attention_sums(0)
                if on[FFN]:
                    dve.wait_ge(filled["f_v3"], F.n + 1)
                    dve.wait_ge(a_["r_tanh_done"], F.n + 1)
                    nc.vector.scalar_tensor_tensor(flat(gated), flat(r_tanh), 1.0, bank_of("v3")[:],
                                                   op0=ALU.add, op1=ALU.mult).then_inc(v_["gated_done"], 1)
                attention_out(0)
                if on[CROSS]:
                    dve.wait_ge(filled["f_z2"], X.n + 1)
                    dve.wait_ge(g_["x1p_ready"], X.n + 1)
                    wait(dve, a_["x2_ready"], X.n)
                    nc.vector.tensor_tensor(flat(sum2), bank_of("z2")[:], flat(x1p), ALU.add) \
                        .then_inc(v_["sum2_done"], 1)
                if on[FFN]:
                    dve.wait_ge(v_["gated_done"], F.n + 1)
                    wait(dve, out_saved, F.n * (16 * NT))
                    nc.vector.scalar_tensor_tensor(flat(sum3), flat(gated), 0.5, flat(x2),
                                                   op0=ALU.mult, op1=ALU.add).then_inc(v_["sum3_done"], 1)
                if on[CROSS]:
                    stats(1, X, sum2, v_["sum2_done"])
                attention_sums(1)
                attention_out(1)

            run_steps(dve, step, ahead=1, late=1, between=other_weights)

        @block.gpsimd
        def _(pool):
            done = [0]

            def link(ins):
                done[0] += 1
                ins.then_inc(consts_step, 1)
                pool.wait_ge(consts_step, done[0])

            g = nc.gpsimd
            link(g.memset(ident[:], 0.0))
            g.affine_select(out=ident[:], in_=ident[:], compare_op=ALU.not_equal, fill=1.0, base=0,
                            pattern=[[-1, P]], channel_multiplier=1).then_inc(ident_ready, 1)
            pool.wait_ge(ident_ready, 1)
            link(g.memset(block_diag, 1.0))
            bd = block_diag.rearrange("p (g e) -> p g e", e=DH)
            link(g.affine_select(out=bd, in_=bd, compare_op=ALU.is_ge, fill=0.0, base=0,
                                 pattern=[[-DH, P // DH], [0, DH]], channel_multiplier=1))
            g.affine_select(out=bd, in_=bd, compare_op=ALU.is_ge, fill=0.0, base=DH - 1,
                            pattern=[[DH, P // DH], [0, DH]], channel_multiplier=-1).then_inc(block_diag_ready, 1)
            for t, value in ((ones_row, 1.0), (neg_half, -0.5), (eps, EPS), (minus_one, -1.0)):
                link(g.memset(t[:], value))
            for r in range(RING):
                for h in range(2):
                    link(g.memset(stack[1][r][64 * h + 32:64 * h + 64].bitcast(F32), 1.0))
            link(g.tensor_copy(identb[:], ident[:]))
            link(g.memset(mask_s[:], 0.0))
            link(g.memset(mask_t[:], 0.0))
            link(g.affine_select(out=mask_s[:], in_=mask_s[:], compare_op=ALU.is_ge, fill=MASKED, base=0,
                                 pattern=[[0, 4], [-1, P]], channel_multiplier=1))
            link(g.affine_select(out=mask_t[:], in_=mask_t[:], compare_op=ALU.is_ge, fill=MASKED, base=0,
                                 pattern=[[0, 4], [1, P]], channel_multiplier=-1))
            g.memset(x2T[:, :, 0:1], 0.0).then_inc(consts_ready, 1)
            pool.wait_ge(setup_taken, SETUP_TOTAL)

            def low_part(c, b):
                pool.wait_ge(p_hi_done[c], b.n + 1)
                i = T_ORDER.index(c)
                g.tensor_tensor(p_lo[c][:], p32[i % 3][:], p_hi[c][:], ALU.subtract).then_inc(p_lo_done[c], 1)

            def inverse_deviation(i, b):
                pool.wait_ge(mv_done[i], b.n + 1)
                wait(pool, (a_["x1_ready"], a_["x2_ready"], x3_ready[1])[i], b.n)
                g.tensor_tensor(var[i][:], mv[i][:, :, 1], eps[:], ALU.add).then_inc(var_done[i], 1)
                g.tensor_tensor(neg_mean[i][:], mv[i][:, :, 0], minus_one[:], ALU.mult).then_inc(neg_mean_done[i], 1)
                pool.wait_ge(var_done[i], b.n + 1)
                g.tensor_tensor(rstd[i][:], var[i][:], neg_half[:], ALU.pow).then_inc(rstd_done[i], 1)
                pool.wait_ge(neg_mean_done[i], b.n + 1)
                pool.wait_ge(rstd_done[i], b.n + 1)
                g.tensor_tensor(offset[i][:], neg_mean[i][:], rstd[i][:], ALU.mult).then_inc(offset_done[i], 1)

            def step(turn, at):
                A, Sb, Pb, X, F = (Batch(turn, at, s) for s in range(5))
                on = [live(turn, at, s) for s in range(5)]
                if on[CROSS]:
                    pool.wait_ge(x_res_loaded, (X.n + 1) * 16)
                    g.tensor_tensor(x_res[:], x_res[:], c1[:].unsqueeze(1).to_broadcast([P, NT, C]), ALU.add) \
                        .then_inc(g_["x_c_ready"], 1)
                if live(turn, at - 1, FFN):
                    inverse_deviation(2, Batch(turn, at - 1, FFN))
                if on[PROBS]:
                    low_part(0, Pb)
                if on[CROSS]:
                    inverse_deviation(0, X)
                if on[FFN]:
                    pool.wait_ge(a_["x2T_ready"], F.n + 1)
                    wait(pool, v_["xr_ready"], F.n)
                    g.tensor_tensor(dx[:], x2T[:, :, 1:1 + T], x2T[:, :, 0:T], ALU.subtract) \
                        .then_inc(g_["dx_done"], 1)
                if on[PROBS]:
                    low_part(2, Pb)
                    low_part(3, Pb)
                if on[FFN]:
                    pool.wait_ge(a_["xr_hi"], F.n + 1)
                    g.tensor_tensor(xr[1][:], xr_f32[:], xr[0][:].bitcast(F32), ALU.subtract) \
                        .then_inc(g_["xr_lo"], 1)
                if on[CROSS]:
                    pool.wait_ge(a_["x1_ready"], X.n + 1)
                    pool.wait_ge(filled["f_x1T"], X.n + 1)
                    g.tensor_tensor(x1p[:], x1[:], pb_rep[:].unsqueeze(1).to_broadcast([P, NT, C]), ALU.add) \
                        .then_inc(g_["x1p_ready"], 1)
                if on[PROBS]:
                    low_part(1, Pb)
                    low_part(4, Pb)
                    low_part(5, Pb)
                if on[SCORES]:
                    pool.wait_ge(a_["v_mid"], Sb.n + 1)
                    for j in range(NT):
                        last = g.tensor_tensor(v_parts[Sb.slot][:, j, :, 2, 0:DH],
                                               v_rest[:, j, :].rearrange("p (h d) -> p h d", h=HEADS),
                                               v_parts[Sb.slot][:, j, :, 1, 0:DH], ALU.subtract)
                    last.then_inc(g_["v_lo"], 1)
                if on[CROSS]:
                    inverse_deviation(1, X)

            run_steps(pool, step, ahead=1, late=1)


SETUP_FIRST = 5
SETUP_TOTAL = SETUP_FIRST + 7 + 3


_INS = ['x', 'ctx_1024', 'mask_S2_ik0', 'L0_attn_Wq', 'L0_attn_bq', 'L0_attn_Wk', 'L0_attn_bk', 'L0_attn_Wv',
        'L0_attn_bv', 'L0_attn_Wo', 'L0_attn_bo', 'L0_attn_Wq_lsr', 'L0_attn_Wk_lsr', 'L0_xattn_qkv_w',
        'L0_xattn_proj_w', 'L0_xattn_proj_b', 'L0_ffn_W_r', 'L0_ffn_W_k', 'L0_ffn_W_v', 'L0_ffn_mu_r', 'L0_ffn_mu_k']


def kernel(**inputs):
    import numpy as np
    import concourse.bacc as bacc
    from concourse import mybir as _mybir
    from concourse.bass_utils import run_bass_kernel_spmd

    nc = bacc.Bacc("TRN2", target_bir_lowering=False, num_devices=1)
    arrays, args = {}, []
    for name in _INS:
        a = np.ascontiguousarray(inputs[name])
        arrays[f"in_{name}"] = a
        args.append(nc.dram_tensor(f"in_{name}", a.shape, _mybir.dt.from_np(a.dtype), kind="ExternalInput").ap())
    shape = np.shape(inputs['x'])
    args.append(nc.dram_tensor("out_x", shape, _mybir.dt.float32, kind="ExternalOutput").ap())
    decoder_layer(nc, *args)
    r = run_bass_kernel_spmd(nc, [arrays], core_ids=[0])
    return r.results[0]["out_x"]
```
